# Optimizing a Trainium2 kernel written in Bass

```python
import numpy as np
import jax
import jax.numpy as jnp

def _softmax(x, axis=-1):
    return jax.nn.softmax(x, axis=axis)

def _gelu(x):
    return jax.nn.gelu(x, approximate=True)

def _silu(x):
    return jax.nn.silu(x)

def _sigmoid(x):
    return jax.nn.sigmoid(x)

def _layernorm(x, axis=-1, eps=1e-05):
    m = jnp.mean(x, axis=axis, keepdims=True)
    v = jnp.var(x, axis=axis, keepdims=True)
    return (x - m) / jnp.sqrt(v + eps)

def _scatter_add(tgt, idx, src, axis=0):
    return tgt.at[idx].add(src)

def _segment_sum(src, seg, n):
    return jax.ops.segment_sum(src, seg, n)
kernel_name = 'mk_flamingo_gated_d2_seqx_r8_8b016d'

def setup_inputs(seed: int=0):
    np.random.seed(seed)
    _w = jnp.asarray

    def _rec_inputs():
        import jax
        import jax.numpy as jnp
        _rk = jax.random.key(seed)
        x = -0.0002928 + 1 * jax.random.normal(jax.random.fold_in(_rk, 1), (32, 128, 128), jnp.float32)
        _lenS = 128 - jax.random.randint(jax.random.fold_in(_rk, 7), (32,), 0, max(1, 128 // 4) + 1, jnp.int32)
        _lenS2 = 77 - jax.random.randint(jax.random.fold_in(_rk, 8), (32,), 0, max(1, 77 // 4) + 1, jnp.int32)
        _ctx_1024P = jax.random.normal(jax.random.fold_in(_rk, 11), (32, 16, 128), jnp.float32)
        _ctx_1024c = jax.random.dirichlet(jax.random.fold_in(_rk, 511), 0.3 * jnp.ones((16,), jnp.float32), (32, 77))
        _ctx_1024t = jnp.einsum('bsk,bkd->bsd', _ctx_1024c, _ctx_1024P)
        _ctx_1024t = _ctx_1024t * jax.lax.rsqrt(jnp.mean(jnp.square(_ctx_1024t)) + 1e-12) * 0.953939
        ctx_1024 = -1.52775e-05 + 0.999936 * (_ctx_1024t + 0.3 * jax.random.normal(jax.random.fold_in(_rk, 611), (32, 77, 128), jnp.float32))
        _g = jax.random.normal(jax.random.fold_in(_rk, 9001), (2, 2), jnp.float32)
        _g = jnp.sign(_g) * jnp.maximum(jnp.abs(_g), 1.0) + (_g == 0) * 1.0
        g_xattn = _g[0]
        g_ffn = _g[1]
        return (x, ctx_1024, g_xattn, g_ffn)
    x, ctx_1024, g_xattn, g_ffn = _rec_inputs()

    def _L0_xattn_setup():
        import jax, jax.numpy as jnp
        import numpy as np
        DIM = 128
        NUM_HEADS = 8
        HEAD_DIM = 64
        INNER = NUM_HEADS * HEAD_DIM
        key = jax.random.key(seed)
        ks = jax.random.split(key, 7)
        B, N, M = (8, 64, 512)
        x = jax.random.normal(ks[0], (B, N, DIM), dtype=jnp.float32)
        context = jax.random.normal(ks[1], (B, M, DIM), dtype=jnp.float32)
        s_in = 1.0 / np.sqrt(DIM)
        s_inner = 1.0 / np.sqrt(INNER)
        Wq = jax.random.normal(ks[2], (DIM, INNER), dtype=jnp.float32) * s_in
        Wk = jax.random.normal(ks[3], (DIM, INNER), dtype=jnp.float32) * s_in
        Wv = jax.random.normal(ks[4], (DIM, INNER), dtype=jnp.float32) * s_in
        Wo = jax.random.normal(ks[5], (INNER, DIM), dtype=jnp.float32) * s_inner
        bo = jax.random.normal(ks[6], (DIM,), dtype=jnp.float32) * 0.01
        return {'x': x, 'context': context, 'Wq': Wq, 'Wk': Wk, 'Wv': Wv, 'Wo': Wo, 'bo': bo}
    _L0_xattn_all = _L0_xattn_setup()
    _L0_xattn_in = {k: v for k, v in _L0_xattn_all.items() if k in ('Wq', 'Wk', 'Wv', 'Wo', 'bo')}
    del _L0_xattn_all

    def _L0_ffn_setup():
        import jax, jax.numpy as jnp
        import numpy as np
        D, H, N, K = (128, 256, 8, 2)
        B, S = (4, 256)
        key = jax.random.key(seed)
        ks = jax.random.split(key, 4)
        x = jax.random.normal(ks[0], (B, S, D), dtype=jnp.float32)
        Wr = jax.random.normal(ks[1], (N, D), dtype=jnp.float32) / np.sqrt(D)
        br = jnp.zeros((N,), jnp.float32)
        Wl1 = jax.random.normal(ks[2], (N, D, 2 * H), dtype=jnp.float32) / np.sqrt(D)
        bl1 = jnp.zeros((N, 2 * H), jnp.float32)
        Wl2 = jax.random.normal(ks[3], (N, H, D), dtype=jnp.float32) / np.sqrt(H)
        bl2 = jnp.zeros((N, D), jnp.float32)
        biases_N = jnp.zeros((N,), jnp.float32)
        return {'x': x, 'Wr': Wr, 'br': br, 'Wl1': Wl1, 'bl1': bl1, 'Wl2': Wl2, 'bl2': bl2, 'biases_N': biases_N}
    _L0_ffn_all = _L0_ffn_setup()
    _L0_ffn_in = {k: v for k, v in _L0_ffn_all.items() if k in ('Wr', 'br', 'Wl1', 'bl1', 'Wl2', 'bl2', 'biases_N')}
    del _L0_ffn_all

    def _L1_xattn_setup():
        import jax, jax.numpy as jnp
        import numpy as np
        D_MODEL = 128
        N_HEADS = 16
        D_K = D_MODEL // N_HEADS
        SCALE = float(np.sqrt(D_K))
        key = jax.random.key(seed)
        ks = jax.random.split(key, 11)
        B, L, D = (2, 256, D_MODEL)
        s = 1.0 / np.sqrt(D)
        inp = {'q': jax.random.normal(ks[0], (B, L, D), dtype=jnp.float32), 'k': jax.random.normal(ks[1], (B, L, D), dtype=jnp.float32), 'v': jax.random.normal(ks[2], (B, L, D), dtype=jnp.float32), 'Wq': jax.random.normal(ks[3], (D, D), dtype=jnp.float32) * s, 'bq': jnp.zeros((D,), dtype=jnp.float32), 'Wk': jax.random.normal(ks[4], (D, D), dtype=jnp.float32) * s, 'bk': jnp.zeros((D,), dtype=jnp.float32), 'Wv': jax.random.normal(ks[5], (D, D), dtype=jnp.float32) * s, 'bv': jnp.zeros((D,), dtype=jnp.float32), 'Wo': jax.random.normal(ks[6], (D, D), dtype=jnp.float32) * s, 'bo': jnp.zeros((D,), dtype=jnp.float32)}
        return inp
    _L1_xattn_all = _L1_xattn_setup()
    _L1_xattn_in = {k: v for k, v in _L1_xattn_all.items() if k in ('Wq', 'bq', 'Wk', 'bk', 'Wv', 'bv', 'Wo', 'bo')}
    del _L1_xattn_all

    def _L1_ffn_setup():
        import jax, jax.numpy as jnp
        import numpy as np
        HIDDEN = 128
        NUM_EXPERTS = 8
        TOP_K = 2
        key = jax.random.key(seed)
        k_x, k_r, k_w1, k_w2 = jax.random.split(key, 4)
        x = jax.random.normal(k_x, (4, 256, HIDDEN), dtype=jnp.float32)
        router_w = jax.random.normal(k_r, (NUM_EXPERTS, HIDDEN), dtype=jnp.float32) * HIDDEN ** (-0.5)
        w1 = jax.random.normal(k_w1, (NUM_EXPERTS, HIDDEN, 2 * HIDDEN), dtype=jnp.float32) * HIDDEN ** (-0.5)
        w2 = jax.random.normal(k_w2, (NUM_EXPERTS, 2 * HIDDEN, HIDDEN), dtype=jnp.float32) * (2 * HIDDEN) ** (-0.5)
        return {'x': x, 'router_w': router_w, 'w1': w1, 'w2': w2}
    _L1_ffn_all = _L1_ffn_setup()
    _L1_ffn_in = {k: v for k, v in _L1_ffn_all.items() if k in ('router_w', 'w1', 'w2')}
    del _L1_ffn_all
    return {'x': x, 'ctx_1024': ctx_1024, 'g_xattn': g_xattn, 'g_ffn': g_ffn, 'L0_xattn_Wq': _L0_xattn_in['Wq'], 'L0_xattn_Wk': _L0_xattn_in['Wk'], 'L0_xattn_Wv': _L0_xattn_in['Wv'], 'L0_xattn_Wo': _L0_xattn_in['Wo'], 'L0_xattn_bo': _L0_xattn_in['bo'], 'L0_ffn_Wr': _L0_ffn_in['Wr'], 'L0_ffn_br': _L0_ffn_in['br'], 'L0_ffn_Wl1': _L0_ffn_in['Wl1'], 'L0_ffn_bl1': _L0_ffn_in['bl1'], 'L0_ffn_Wl2': _L0_ffn_in['Wl2'], 'L0_ffn_bl2': _L0_ffn_in['bl2'], 'L0_ffn_biases_N': _L0_ffn_in['biases_N'], 'L1_xattn_Wq': _L1_xattn_in['Wq'], 'L1_xattn_bq': _L1_xattn_in['bq'], 'L1_xattn_Wk': _L1_xattn_in['Wk'], 'L1_xattn_bk': _L1_xattn_in['bk'], 'L1_xattn_Wv': _L1_xattn_in['Wv'], 'L1_xattn_bv': _L1_xattn_in['bv'], 'L1_xattn_Wo': _L1_xattn_in['Wo'], 'L1_xattn_bo': _L1_xattn_in['bo'], 'L1_ffn_router_w': _L1_ffn_in['router_w'], 'L1_ffn_w1': _L1_ffn_in['w1'], 'L1_ffn_w2': _L1_ffn_in['w2']}

def reference(x, ctx_1024, g_xattn, g_ffn, L0_xattn_Wq, L0_xattn_Wk, L0_xattn_Wv, L0_xattn_Wo, L0_xattn_bo, L0_ffn_Wr, L0_ffn_br, L0_ffn_Wl1, L0_ffn_bl1, L0_ffn_Wl2, L0_ffn_bl2, L0_ffn_biases_N, L1_xattn_Wq, L1_xattn_bq, L1_xattn_Wk, L1_xattn_bk, L1_xattn_Wv, L1_xattn_bv, L1_xattn_Wo, L1_xattn_bo, L1_ffn_router_w, L1_ffn_w1, L1_ffn_w2):
    import jax
    import jax.numpy as jnp

    def _L0_xattn_ref(x, context, Wq, Wk, Wv, Wo, bo):
        import jax, jax.numpy as jnp
        import numpy as np
        DIM = 128
        NUM_HEADS = 8
        HEAD_DIM = 64
        INNER = NUM_HEADS * HEAD_DIM
        B, N, _ = x.shape
        M = context.shape[1]
        scale = HEAD_DIM ** (-0.5)
        q = (x @ Wq).reshape(B, N, NUM_HEADS, HEAD_DIM).transpose(0, 2, 1, 3)
        k = (context @ Wk).reshape(B, M, NUM_HEADS, HEAD_DIM).transpose(0, 2, 1, 3)
        v = (context @ Wv).reshape(B, M, NUM_HEADS, HEAD_DIM).transpose(0, 2, 1, 3)
        attn = jax.nn.softmax(jnp.einsum('bhnd,bhmd->bhnm', q, k) * scale, axis=-1)
        out = jnp.einsum('bhnm,bhmd->bhnd', attn, v)
        out = out.transpose(0, 2, 1, 3).reshape(B, N, INNER)
        return out @ Wo + bo

    def _L0_ffn_ref(x, Wr, br, Wl1, bl1, Wl2, bl2, biases_N):
        import jax, jax.numpy as jnp
        import numpy as np
        D, H, N, K = (128, 256, 8, 2)
        B, S = (4, 256)
        Bb, Ss, Dd = x.shape
        scores_BSN = jnp.einsum('bsd,nd->bsn', x, Wr) + br
        w_BSN = jax.nn.softmax(scores_BSN, axis=-1)
        _, idx_BSK = jax.lax.top_k(scores_BSN + biases_N[None, None, :], K)
        val_BSK = jnp.take_along_axis(w_BSN, idx_BSK, axis=-1)
        val_BSK = val_BSK / jnp.sum(val_BSK, axis=-1, keepdims=True)
        M = Bb * Ss
        x_MD = x.reshape(M, Dd)
        idx_MK = idx_BSK.reshape(M, K)
        val_MK = val_BSK.reshape(M, K)
        h_NM2H = jnp.einsum('md,ndh->nmh', x_MD, Wl1) + bl1[:, None, :]
        a_NMH, b_NMH = (h_NM2H[..., :H], h_NM2H[..., H:])
        y_NMD = jnp.einsum('nmh,nhd->nmd', jax.nn.silu(a_NMH) * b_NMH, Wl2) + bl2[:, None, :]
        ew_MN = jnp.zeros((M, N), x.dtype)
        ew_MN = ew_MN.at[jnp.arange(M)[:, None], idx_MK].set(val_MK)
        y_MD = jnp.einsum('mn,nmd->md', ew_MN, y_NMD)
        return y_MD.reshape(Bb, Ss, Dd)

    def _L1_xattn_ref(q, k, v, Wq, bq, Wk, bk, Wv, bv, Wo, bo):
        import jax, jax.numpy as jnp
        import numpy as np
        D_MODEL = 128
        N_HEADS = 16
        D_K = D_MODEL // N_HEADS
        SCALE = float(np.sqrt(D_K))
        B, L, D = q.shape
        H, Dk = (N_HEADS, D_K)

        def proj(x, W, b):
            y = x @ W + b
            return y.reshape(B, -1, H, Dk).transpose(0, 2, 1, 3)
        qh = proj(q, Wq, bq)
        kh = proj(k, Wk, bk)
        vh = proj(v, Wv, bv)
        scores = jnp.einsum('bhqd,bhkd->bhqk', qh, kh) / SCALE
        attn = jax.nn.softmax(scores, axis=-1)
        out = jnp.einsum('bhqk,bhkd->bhqd', attn, vh)
        out = out.transpose(0, 2, 1, 3).reshape(B, -1, D)
        return out @ Wo + bo

    def _L1_ffn_ref(x, router_w, w1, w2):
        import jax, jax.numpy as jnp
        import numpy as np
        HIDDEN = 128
        NUM_EXPERTS = 8
        TOP_K = 2
        bsz, seq, hidden = x.shape
        tokens = x.reshape(-1, hidden)
        logits = tokens @ router_w.T
        topk_vals, topk_idx = jax.lax.top_k(logits, TOP_K)
        weights = jax.nn.softmax(topk_vals, axis=-1)
        h = jnp.einsum('td,edf->etf', tokens, w1)
        h = jax.nn.gelu(h, approximate=False)
        out_all = jnp.einsum('etf,efd->etd', h, w2)
        out_ted = jnp.transpose(out_all, (1, 0, 2))
        gathered = jnp.take_along_axis(out_ted, topk_idx[:, :, None], axis=1)
        output = jnp.sum(weights[:, :, None] * gathered, axis=1)
        return output.reshape(bsz, seq, hidden)
    x = x + jnp.tanh(g_xattn[0]) * _L0_xattn_ref(_layernorm(x, axis=-1), ctx_1024, L0_xattn_Wq, L0_xattn_Wk, L0_xattn_Wv, L0_xattn_Wo, L0_xattn_bo)
    x = x + jnp.tanh(g_ffn[0]) * _L0_ffn_ref(_layernorm(x, axis=-1), L0_ffn_Wr, L0_ffn_br, L0_ffn_Wl1, L0_ffn_bl1, L0_ffn_Wl2, L0_ffn_bl2, L0_ffn_biases_N)
    x = x + jnp.tanh(g_xattn[1]) * _L1_xattn_ref(_layernorm(x, axis=-1), ctx_1024, ctx_1024, L1_xattn_Wq, L1_xattn_bq, L1_xattn_Wk, L1_xattn_bk, L1_xattn_Wv, L1_xattn_bv, L1_xattn_Wo, L1_xattn_bo)
    x = x + jnp.tanh(g_ffn[1]) * _L1_ffn_ref(_layernorm(x, axis=-1), L1_ffn_router_w, L1_ffn_w1, L1_ffn_w2)
    return x

_drawn_inputs = setup_inputs


def setup_inputs(seed=0):
    import zlib

    import numpy as np

    out = dict(_drawn_inputs(seed))
    spreads = {'g_ffn': (-1.0, 0.6),
     'L0_ffn_br': (0.0, 0.1),
     'L0_ffn_bl1': (0.0, 0.1),
     'L0_ffn_bl2': (0.0, 0.1),
     'L0_ffn_biases_N': (0.0, 0.1),
     'L1_xattn_bq': (0.0, 0.1),
     'L1_xattn_bk': (0.0, 0.8),
     'L1_xattn_bv': (0.0, 0.1),
     'L1_xattn_bo': (0.0, 0.1)}
    factors = {}
    for name, (base, spread) in spreads.items():
        noise = np.random.default_rng([zlib.crc32(name.encode()), seed]).standard_normal(out[name].shape)
        drawn = base * np.exp(spread * noise) if base else spread * noise
        out[name] = jnp.asarray(drawn.astype(out[name].dtype))
    for name, factor in factors.items():
        out[name] = (out[name] * factor).astype(out[name].dtype)
    return out
```

```python
from contextlib import ExitStack

import concourse.bass as bass
from concourse import mybir

ALU = mybir.AluOpType
ACT = mybir.ActivationFunctionType
AX = mybir.AxisListType
F32 = mybir.dt.float32
F32R = mybir.dt.float32r
U32 = mybir.dt.uint32

P = 128
EPS = 1e-5
PSUM_BANK = 512
PSUM_BANKS = 8


class Lane:

    def __init__(self, name, counts, semaphore):
        self.name, self.counts, self.semaphore = name, counts, semaphore
        self.steps, self.waited = [], {}

    def wait(self, *tickets):
        for ticket in tickets:
            if ticket is not None and self.waited.get(ticket[0], 0) < ticket[1]:
                self.waited[ticket[0]] = ticket[1]
                self.steps.append(("wait", *ticket, 0))

    def run(self, emit, *tickets, signal=None, by=1):
        self.wait(*tickets)
        self.steps.append(("do", emit, signal, by))
        if signal is None:
            return None
        self.semaphore(signal)
        self.counts[signal] = self.counts.get(signal, 0) + by
        return signal, self.counts[signal]

    def play(self, eng):
        for kind, what, arg, by in self.steps:
            if kind == "wait":
                eng.wait_ge(self.semaphore(what), arg)
            else:
                ins = what(eng)
                if arg is not None:
                    ins.then_inc(self.semaphore(arg), by)


def flamingo_two_layers(nc, a, out):
    x_dram, ctx_dram = a["x"], a["ctx_1024"]
    NSEQ, SEQ, D = x_dram.shape
    _, NKEY, _ = ctx_dram.shape
    INNER0 = a["L0_xattn_Wq"].shape[1]
    NEXP, _, TWOH0 = a["L0_ffn_Wl1"].shape
    HID1 = a["L1_ffn_w1"].shape[2]
    DK0, DK1 = 64, 8
    NH0, NH1 = INNER0 // DK0, D // DK1
    GS = 4
    NG = NSEQ // GS
    GT = GS * SEQ
    GK = GS * NKEY
    CTX_ROWS = NSEQ * NKEY
    CTX_BLOCKS = (CTX_ROWS + P - 1) // P
    ROW1 = 32
    UH = 8
    assert SEQ == P and D == P and GT == PSUM_BANK and NH0 == UH and NH1 == 2 * UH
    assert TWOH0 == 4 * P and HID1 == 2 * P and NEXP == 8

    with ExitStack() as stack:
        def sbuf(name, shape, dt=F32):
            return stack.enter_context(nc.sbuf_tensor(name, shape, dt))

        semaphores = {}

        def semaphore(name):
            if name not in semaphores:
                semaphores[name] = stack.enter_context(nc.semaphore(name))
            return semaphores[name]

        counts = {}
        sync = Lane("sync", counts, semaphore)
        pe = Lane("pe", counts, semaphore)
        act = Lane("act", counts, semaphore)
        dve = Lane("dve", counts, semaphore)
        pool = Lane("pool", counts, semaphore)

        def load(lane, dst, src, name, scattered=False):
            return lane.run(lambda e: e.dma_start(dst, src, allow_slow_non_contiguous=scattered),
                            signal="in_" + name, by=16)

        x_res = sbuf("x_res", [P, NSEQ, D])
        ident = sbuf("ident", [P, P])
        iota8 = sbuf("iota8", [P, NEXP])
        gates_raw = sbuf("gates_raw", [P, 4])
        gates = sbuf("gates", [P, 4])
        minus_half = sbuf("minus_half", [P, GS])
        ctx_t = sbuf("ctx_t", [P, CTX_ROWS])
        ctx_th = sbuf("ctx_th", [P, CTX_ROWS], F32R)
        ctx_tl = sbuf("ctx_tl", [P, CTX_ROWS], F32R)

        wq_h = [sbuf(f"wq{l}_h", [P, 4, P], F32R) for l in (0, 1)]
        wq_l = [sbuf(f"wq{l}_l", [P, 4, P], F32R) for l in (0, 1)]
        wk_h = [sbuf(f"wk{l}_h", [P, 4, P], F32R) for l in (0, 1)]
        wk_l = [sbuf(f"wk{l}_l", [P, 4, P], F32R) for l in (0, 1)]
        wv0_h = sbuf("wv0_h", [P, INNER0], F32R)
        wv0_l = sbuf("wv0_l", [P, INNER0], F32R)
        wv1 = sbuf("wv1", [P, D])
        wo = [sbuf("wo0", [P, 4, D]), sbuf("wo1", [P, 1, D])]
        bq1 = sbuf("bq1", [P, 4])
        bk1 = sbuf("bk1", [P, 4])
        bv1 = sbuf("bv1", [NKEY, D])
        bo = [sbuf("bo0", [P, D]), sbuf("bo1", [P, D])]

        up_h = sbuf("up_h", [P, NEXP, TWOH0], F32R)
        up_l = sbuf("up_l", [P, NEXP, TWOH0], F32R)
        down = [sbuf("down0", [P, NEXP, 2, D]), sbuf("down1", [P, NEXP, 2, D])]
        up_bias = sbuf("up_bias", [P, NEXP, 4])
        down_bias = sbuf("down_bias", [P, D])
        router = [sbuf(f"router{l}", [P, NEXP]) for l in (0, 1)]
        router_h = [sbuf(f"router{l}_h", [P, NEXP], F32R) for l in (0, 1)]
        router_l = [sbuf(f"router{l}_l", [P, NEXP], F32R) for l in (0, 1)]
        router_b = sbuf("router_b", [P, NEXP])
        select_b = sbuf("select_b", [P, NEXP])

        stats = sbuf("stats", [P, 2, GS, 6])
        mean_var = sbuf("mean_var", [P, 2, GS, 2])
        rstd = sbuf("rstd", [P, 2, GS])
        x_norm = sbuf("x_norm", [P, 2, GS, D])
        xt_h = sbuf("xt_h", [P, 2, GT], F32R)
        xt_l = sbuf("xt_l", [P, 2, GT], F32R)

        q_t = sbuf("q_t", [P, 2, 4, GT])
        k_t = sbuf("k_t", [P, 2, 4, GK])
        v0 = sbuf("v0", [NKEY, 2, NH0, DK0 + 1])
        v1 = sbuf("v1", [NKEY, 2, NH1, DK1 + 1])
        prob = sbuf("prob", [P, 2, UH, NKEY])
        prob_t = sbuf("prob_t", [NKEY, 2, UH, SEQ])
        row_max = sbuf("row_max", [P, 2, UH])
        inv_sum = sbuf("inv_sum", [P, 2, NH1])
        o_sb = sbuf("o_sb", [P, 2, INNER0])
        o_t = sbuf("o_t", [P, 2, 4, SEQ])

        scores = sbuf("scores", [P, 2, GS, NEXP])
        ranked = sbuf("ranked", [P, 2, GS, NEXP])
        top_val = sbuf("top_val", [P, 2, GS, 8])
        top_idx = sbuf("top_idx", [P, 2, GS, 8], U32)
        top_idf = sbuf("top_idf", [P, 2, GS, 2])
        hot1 = sbuf("hot1", [P, 2, GS, NEXP])
        hot2 = sbuf("hot2", [P, 2, GS, NEXP])
        hot_d = sbuf("hot_d", [P, 2, GS, NEXP])
        hot_s = sbuf("hot_s", [P, 2, GS, NEXP])
        lead = sbuf("lead", [P, 2, GS])
        lead_w = sbuf("lead_w", [P, 2, GS])
        ew = sbuf("ew", [P, 2, GS, 32])
        ew_t = sbuf("ew_t", [P, 2, P])
        acted = sbuf("acted", [P, 2, 2, GT])
        hidden = sbuf("hidden", [P, 2, 2, GT])
        up_raw = sbuf("up_raw", [P, 2, TWOH0])

        banks = stack.enter_context(nc.psum_tensor("banks", [P, PSUM_BANKS, PSUM_BANK], F32))

        def past(tickets, n, *rest, first=None):
            return first if n < 0 else tickets[(n, *rest) if rest else n]

        def split_weight(lane, name, stage, hi, lo, *after):
            th = lane.run(lambda e: e.tensor_copy(hi, stage), *after, signal=name + "_hi")
            return lane.run(lambda e: e.tensor_tensor(lo, stage, hi.bitcast(F32), ALU.subtract), th,
                            signal=name + "_lo")

        raw = [view[:, i, j, :] for view in (acted, hidden) for i in (0, 1) for j in (0, 1)]
        t_ctx = []
        ctx_flat = ctx_dram.rearrange("b k d -> (b k) d")
        full_blocks = CTX_ROWS // P
        ctx_stage = q_t[:, :, :, :].rearrange("p a b c -> p (a b c)").rearrange("p (n d) -> p n d", d=D)
        t_x = []
        xg = x_dram.rearrange("b p d -> p b d")
        t_x.append(load(sync, x_res[:, 0:GS, :], xg[:, 0:GS, :], "x0"))
        t_ctx_full = load(act, ctx_stage[:, 0:full_blocks, :],
                          ctx_flat[0:full_blocks * P, :].rearrange("(n p) d -> p n d", p=P), "ctx")
        tail = CTX_ROWS - full_blocks * P
        t_ctx_tail = load(act, ctx_stage[0:tail, full_blocks, :], ctx_flat[full_blocks * P:, :], "ctx_tail")
        raw_w = {}
        t_raw = {}
        for slot, (name, src) in enumerate((("wq0", a["L0_xattn_Wq"]), ("wk0", a["L0_xattn_Wk"]),
                                            ("wv0", a["L0_xattn_Wv"]))):
            raw_w[name] = raw[slot]
            t_raw[name] = load(sync, raw_w[name], src, name)
        t_gates_x = load(sync, gates_raw[:, 0:2], a["g_xattn"].partition_broadcast(P), "g_xattn")
        t_gates_f = load(sync, gates_raw[:, 2:4], a["g_ffn"].partition_broadcast(P), "g_ffn")
        t_bo = [load(sync, bo[l][:, :], a[f"L{l}_xattn_bo"].partition_broadcast(P), f"bo{l}") for l in (0, 1)]
        t_wo = [load(sync, wo[l][:, :, :], a[f"L{l}_xattn_Wo"].rearrange("(t p) n -> p t n", p=P), f"wo{l}")
                for l in (0, 1)]
        for g in range(1, NG):
            t_x.append(load(sync, x_res[:, g * GS:(g + 1) * GS, :], xg[:, g * GS:(g + 1) * GS, :], f"x{g}"))
        for slot, name in ((3, "Wq"), (4, "Wk")):
            key = name.lower() + "1"
            raw_w[key] = raw[slot][:, 0:D]
            t_raw[key] = load(sync, raw_w[key], a[f"L1_xattn_{name}"], key)
        t_wv1 = load(sync, wv1[:, :], a["L1_xattn_Wv"], "wv1")
        t_bv1 = load(sync, bv1[:, :], a["L1_xattn_bv"].partition_broadcast(NKEY), "bv1")

        t_ident0 = pool.run(lambda e: e.memset(ident[:, :], 0.0), signal="ident")
        t_ident = pool.run(lambda e: e.affine_select(
            out=ident[:, :], in_=ident[:, :], compare_op=ALU.not_equal, fill=1.0, base=0,
            pattern=[[-1, P]], channel_multiplier=1), t_ident0, signal="ident")
        t_mhalf = pool.run(lambda e: e.memset(minus_half[:, :], -0.5), signal="constants")
        t_const = t_mhalf
        for e8 in range(NEXP):
            t_const = pool.run(lambda e, e8=e8: e.memset(iota8[:, e8:e8 + 1], float(e8)), signal="constants")
        for t in (v0[:, :, :, DK0:], v1[:, :, :, DK1:]):
            t_const = pool.run(lambda e, t=t: e.memset(t, 1.0), signal="constants")
        t_const = pool.run(lambda e: e.memset(ew[:, :, :, :], 0.0), signal="constants")
        t_zero1 = pool.run(lambda e: e.memset(bq1[:, :], 0.0), signal="bias_zero")
        t_zero1 = pool.run(lambda e: e.memset(bk1[:, :], 0.0), signal="bias_zero")
        t_bqk1 = []
        for i in range(4):
            for name, dst in (("bq", bq1), ("bk", bk1)):
                src = a[f"L1_xattn_{name}"].rearrange("(b i d) -> i d b", i=4, d=DK1)[i]
                t_bqk1.append(sync.run(lambda e, dst=dst, i=i, src=src: e.dma_start(
                    dst[ROW1 * i:ROW1 * i + DK1, :], src, allow_slow_non_contiguous=True), t_zero1, signal="in_bqk1", by=16))
        t_bqk1 = t_bqk1[-1]

        t_g0 = act.run(lambda e: e.activation(gates[:, :], gates_raw[:, :], ACT.Tanh), t_gates_x, t_gates_f,
                       signal="gates")
        t_bo_g = [pool.run(lambda e, l=l: e.tensor_scalar(bo[l][:, :], bo[l][:, :], gates[:, l:l + 1], None,
                                                          ALU.mult), t_g0, t_bo[l], signal="bo_gated")
                  for l in (0, 1)]

        GEN = (6, 7)
        gen_free = {6: None, 7: None}
        gen_turn = [0]

        def gen_bank():
            n = GEN[gen_turn[0] % 2]
            gen_turn[0] += 1
            return n, gen_free[n]

        t_ctx_t = []
        for first in range(0, CTX_BLOCKS, 4):
            n, free = gen_bank()
            last = min(first + 4, CTX_BLOCKS)
            for j in range(first, last):
                rows = min(P, CTX_ROWS - j * P)
                t = pe.run(lambda e, j=j, rows=rows, n=n, first=first: e.transpose(
                    banks[:, n, (j - first) * P:(j - first) * P + rows], ctx_stage[0:rows, j, :],
                    ident[0:rows, 0:rows]), free, t_ident, t_ctx_full, t_ctx_tail,
                    signal="ctx_transposed" if j == last - 1 else None)
            c0, c1 = first * P, min(last * P, CTX_ROWS)
            t_full = act.run(lambda e, n=n, c0=c0, c1=c1: e.activation(ctx_t[:, c0:c1], banks[:, n, 0:c1 - c0],
                                                                       ACT.Copy), t, signal="ctx_t")
            gen_free[n] = t_full
            t_ctx_t.append(split_weight(dve, "ctx_split", ctx_t[:, c0:c1], ctx_th[:, c0:c1], ctx_tl[:, c0:c1],
                                        t_full))
        t_ctx_all_transposed = t

        def ctx_ready(row_end):
            return t_ctx_t[min((row_end - 1) // (4 * P), len(t_ctx_t) - 1)]

        t_w = {}
        for name, hi, lo, lane in (("wq0", wq_h[0], wq_l[0], pool), ("wk0", wk_h[0], wk_l[0], dve)):
            t_w[name] = split_weight(lane, name, raw_w[name].rearrange("p (a b) -> p a b", a=4),
                                     hi[:, :, :], lo[:, :, :], t_raw[name])
        t_w["wv0"] = split_weight(dve, "wv0", raw_w["wv0"], wv0_h[:, :], wv0_l[:, :], t_raw["wv0"])

        def split_layer1_attention_weights():
            for name, hi, lo, slot in (("wq1", wq_h[1], wq_l[1], 5), ("wk1", wk_h[1], wk_l[1], 6)):
                wide = raw[slot].rearrange("p (b i r) -> p b i r", b=4, i=4)
                tz = pool.run(lambda e, wide=wide: e.memset(wide, 0.0), signal=name + "_wide")
                src = raw_w[name].rearrange("p (b i d) -> p b i d", b=4, i=4)
                tc = pool.run(lambda e, wide=wide, src=src: e.tensor_copy(wide[:, :, :, 0:DK1], src), tz,
                              t_raw[name], signal=name + "_wide")
                t_w[name] = split_weight(pool, name, raw[slot].rearrange("p (a b) -> p a b", a=4),
                                         hi[:, :, :], lo[:, :, :], tc)

        up_raw_free = {}
        t_up = {}
        t_small = {}

        def load_experts(layer, after):
            width = TWOH0 if layer == 0 else HID1
            src_up = a["L0_ffn_Wl1"] if layer == 0 else a["L1_ffn_w1"]
            src_down = a["L0_ffn_Wl2"] if layer == 0 else a["L1_ffn_w2"]
            t_small["down", layer] = load(sync, down[layer][:, :, :, :],
                                          src_down.rearrange("e (t p) d -> p e t d", p=P), f"down{layer}")
            src_router = a["L0_ffn_Wr"] if layer == 0 else a["L1_ffn_router_w"]
            t_r = load(sync, router[layer][:, :], src_router.rearrange("n d -> d n"), f"router{layer}",
                       scattered=True)
            t_small["router", layer] = split_weight(pool, f"router{layer}", router[layer][:, :],
                                                    router_h[layer][:, :], router_l[layer][:, :], t_r)
            if layer == 0:
                load(sync, up_bias[:, :, :], a["L0_ffn_bl1"].rearrange("e (t p) -> p e t", p=P), "moe_bias",
                     scattered=True)
                for i in range(4):
                    load(sync, down_bias[32 * i:32 * i + NEXP, :], a["L0_ffn_bl2"], "moe_bias")
                load(sync, router_b[:, :], a["L0_ffn_br"].partition_broadcast(P), "moe_bias")
                t_small["bias"] = load(sync, select_b[:, :], a["L0_ffn_biases_N"].partition_broadcast(P),
                                       "moe_bias")
            for e8 in range(NEXP):
                slot = e8 % 2
                stage = up_raw[:, slot, 0:width]
                first_after = up_raw_free.get(slot)
                t_in = sync.run(lambda e, stage=stage, e8=e8: e.dma_start(stage, src_up[e8]), first_after,
                                *(after if e8 == 0 else ()), signal=f"in_up_slot{slot}", by=16)
                t_up[layer, e8] = split_weight(pool, "up_split", stage, up_h[:, e8, 0:width],
                                               up_l[:, e8, 0:width], t_in, *(after if e8 == 0 else ()))
                up_raw_free[slot] = t_up[layer, e8]


        x_ready = {b: t_x[b // GS] for b in range(NSEQ)}
        x_read = {b: None for b in range(NSEQ)}
        xt_done = {0: None, 1: None}
        xt_ready = {}
        norm_turn = [0]

        def layernorm_group(g, keep=None):
            s = norm_turn[0] % 2
            norm_turn[0] += 1
            for j in range(GS):
                b = g * GS + j
                t = dve.run(lambda e, b=b, j=j: e.bn_stats(stats[:, s, j, :], x_res[:, b, :]), x_ready[b],
                            signal="ln_stats")
            for j in range(GS):
                t = dve.run(lambda e, j=j: e.bn_aggr(mean_var[:, s, j, :], stats[:, s, j, :]), t, ln_free[s],
                            signal="ln_mean_var")
            t_eps = pool.run(lambda e: e.tensor_scalar(rstd[:, s, :], mean_var[:, s, :, 1], EPS, None, ALU.add),
                             t, ln_free[s], signal="ln_eps")
            t_rstd = pool.run(lambda e: e.tensor_tensor(rstd[:, s, :], rstd[:, s, :], minus_half[:, :], ALU.pow),
                              t_eps, t_mhalf, signal="ln_rstd")
            for j in range(GS):
                b = g * GS + j
                t = pool.run(lambda e, b=b, j=j: e.tensor_scalar(
                    x_norm[:, s, j, :], x_res[:, b, :], mean_var[:, s, j, 0:1], rstd[:, s, j:j + 1],
                    ALU.subtract, ALU.mult), t_rstd, x_ready[b], signal="ln_out")
                x_read[b] = t
            t_norm = t
            ln_free[s] = t
            n, free = gen_bank()
            for j in range(GS):
                t = pe.run(lambda e, j=j: e.transpose(banks[:, n, j * P:(j + 1) * P], x_norm[:, s, j, :],
                                                      ident[:, :]), t_norm, free, t_ident,
                           signal="ln_transposed" if j == GS - 1 else None)
            ln_free[s] = t
            t_h = act.run(lambda e: e.activation(xt_h[:, s, :], banks[:, n, :], ACT.Copy), t, xt_done[s],
                          signal="xt_h")
            t_l = dve.run(lambda e: e.tensor_tensor(xt_l[:, s, :], banks[:, n, :], xt_h[:, s, :].bitcast(F32),
                                                    ALU.subtract), t_h, xt_done[s], signal="xt_l")
            gen_free[n] = t_l
            xt_ready[s] = (t_h, t_l)
            return s

        ln_free = {0: None, 1: None}

        def three_pass(outp, wh, wl, xh, xl, tickets, signal):
            pe.run(lambda e: e.matmul(outp, wh, xh, start=True, stop=False), *tickets)
            pe.run(lambda e: e.matmul(outp, wl, xh, start=False, stop=False))
            return pe.run(lambda e: e.matmul(outp, wh, xl, start=False, stop=True), signal=signal)

        S_BANK = (0, 1)
        PT_BANK = (2, 3)
        O_BANK = (4, 5)

        def attention(layer, state):
            DK = (DK0, DK1)[layer]
            NH = (NH0, NH1)[layer]
            DV1 = DK + 1
            ROWT = (DK0, ROW1)[layer]
            HALVES = NH // UH
            v_sb = (v0, v1)[layer]
            SCALE = float(DK) ** -0.5
            nblk_o = (4, 1)[layer]

            def heads(half):
                for place in range(4):
                    for k in (0, 1):
                        if layer == 0:
                            yield k * 4 + place, 2 * place + k, place, DK0 * k, k, place
                        else:
                            i = 2 * half + k
                            yield k * 4 + place, 4 * place + i, place, ROW1 * i, k, place

            units = [(b, h) for b in range(NSEQ) for h in range(HALVES)]
            q_ready, k_ready, v_ready = {}, {}, {}
            scores_done = {}
            pv_done, prob_t_read = {}, {}
            sub_done, exp_done, pt_done, pt_copied, norm_done, ot_ready, y_done = {}, {}, {}, {}, {}, {}, {}
            ot_read = {}
            last_unit = lambda b: b * HALVES + HALVES - 1
            slot_of = {}

            def q_block(g, blk):
                s = slot_of[g]
                n, free = gen_bank()
                old = past(scores_done, last_unit(g * GS - GS - 1) if g >= 2 else -1, first=state["q_free"])
                t = three_pass(banks[:, n, :], wq_h[layer][:, blk, :], wq_l[layer][:, blk, :],
                               xt_h[:, s, :], xt_l[:, s, :], (free, *xt_ready[s], t_w[f"wq{layer}"]), "q_proj")
                if blk == 3:
                    xt_done[s] = t
                if layer == 0:
                    t = act.run(lambda e: e.activation(q_t[:, g % 2, blk, :], banks[:, n, :], ACT.Copy), t, old,
                                signal="q_t")
                else:
                    t = act.run(lambda e: e.activation(q_t[:, g % 2, blk, :], banks[:, n, :], ACT.Identity,
                                                       bias=bq1[:, blk:blk + 1]), t, old, t_bqk1, signal="q_t")
                gen_free[n] = t
                q_ready[g] = t

            def k_block(g, blk):
                c0 = g * GK
                n, free = gen_bank()
                old = past(scores_done, last_unit(g * GS - GS - 1) if g >= 2 else -1, first=state["q_free"])
                t = three_pass(banks[:, n, 0:GK], wk_h[layer][:, blk, :], wk_l[layer][:, blk, :],
                               ctx_th[:, c0:c0 + GK], ctx_tl[:, c0:c0 + GK],
                               (free, ctx_ready(c0 + GK), t_w[f"wk{layer}"]), "k_proj")
                if layer == 0:
                    t = act.run(lambda e: e.activation(k_t[:, g % 2, blk, :], banks[:, n, 0:GK], ACT.Copy), t, old,
                                signal="k_t")
                else:
                    t = act.run(lambda e: e.activation(k_t[:, g % 2, blk, :], banks[:, n, 0:GK], ACT.Identity,
                                                       bias=bk1[:, blk:blk + 1]), t, old, t_bqk1, signal="k_t")
                gen_free[n] = t
                k_ready[g] = t

            def v_proj(b):
                c0 = b * NKEY
                n, free = gen_bank()
                old = past(pv_done, last_unit(b - 2) if b >= 2 else -1)
                if layer == 0:
                    t = three_pass(banks[0:NKEY, n, :], ctx_th[:, c0:c0 + NKEY], ctx_tl[:, c0:c0 + NKEY],
                                   wv0_h[:, :], wv0_l[:, :], (free, ctx_ready(c0 + NKEY), t_w["wv0"]), "v_proj")
                    t = dve.run(lambda e: e.tensor_copy(
                        v0[:, b % 2, :, 0:DK0], banks[0:NKEY, n, :].rearrange("p (h d) -> p h d", d=DK0)),
                        t, old, signal="v")
                else:
                    t = pe.run(lambda e: e.matmul(banks[0:NKEY, n, 0:D], ctx_t[:, c0:c0 + NKEY], wv1[:, :],
                                                  start=True, stop=True), free, ctx_ready(c0 + NKEY), t_wv1,
                               signal="v_proj")
                    t = dve.run(lambda e: e.tensor_tensor(
                        v1[:, b % 2, :, 0:DK1], banks[0:NKEY, n, 0:D].rearrange("p (h d) -> p h d", d=DK1),
                        bv1[:, :].rearrange("p (h d) -> p h d", d=DK1), ALU.add), t, old, t_bv1, signal="v")
                gen_free[n] = t
                v_ready[b] = t

            def score(u):
                b, half = units[u]
                g, j = b // GS, b % GS
                for slot, head, blk, row, k, place in heads(half):
                    t = pe.run(lambda e, blk=blk, row=row, k=k, place=place: e.matmul(
                        banks[:, S_BANK[k], place * NKEY:(place + 1) * NKEY],
                        q_t[row:row + ROWT, g % 2, blk, j * SEQ:(j + 1) * SEQ],
                        k_t[row:row + ROWT, g % 2, blk, j * NKEY:(j + 1) * NKEY],
                        start=True, stop=True, tile_position=(row, 0)),
                        q_ready[g], k_ready[g], past(sub_done, u - 1, first=state["s_free"]),
                        signal="scores" if (slot % 4, k) == (3, 1) else None)
                scores_done[u] = t
                s_view = banks[:, S_BANK[0]:S_BANK[1] + 1, 0:4 * NKEY].rearrange("p k (s n) -> p k s n", n=NKEY)
                m_view = row_max[:, u % 2, :].rearrange("p (k s) -> p k s", k=2)
                p_view = prob[:, u % 2, :, :].rearrange("p (k s) n -> p k s n", k=2)
                t = dve.run(lambda e: e.tensor_reduce(m_view, s_view, AX.X, ALU.max), t, signal="row_max")
                t = dve.run(lambda e: e.tensor_tensor(
                    p_view, s_view, m_view.unsqueeze(3).to_broadcast([P, 2, 4, NKEY]), ALU.subtract), t,
                    past(pt_done, u - 2), signal="shifted")
                sub_done[u] = t
                exp_done[u] = act.run(lambda e: e.activation(prob[:, u % 2, :, :], prob[:, u % 2, :, :], ACT.Exp,
                                                             scale=SCALE), t, signal="exp")

            def transpose_prob(u):
                for k in (0, 1):
                    for place in range(4):
                        t = pe.run(lambda e, k=k, place=place: e.transpose(
                            banks[0:NKEY, PT_BANK[k], place * SEQ:(place + 1) * SEQ],
                            prob[:, u % 2, 4 * k + place, :], ident[:, :]),
                            exp_done[u], past(pt_copied, u - 1, k, first=state["pt_free"][k]),
                            signal="prob_transposed" if place == 3 else None)
                    dst = prob_t[:, u % 2, 4 * k:4 * k + 4, :].rearrange("p s n -> p (s n)")
                    if k == 0 or (layer == 1 and u % 2 == 0):
                        pt_copied[u, k] = act.run(lambda e, dst=dst, k=k: e.activation(
                            dst, banks[0:NKEY, PT_BANK[k], :], ACT.Copy), t, past(pv_done, u - 2), signal="prob_t_act")
                    else:
                        pt_copied[u, k] = dve.run(lambda e, dst=dst, k=k: e.tensor_copy(
                            dst, banks[0:NKEY, PT_BANK[k], :]), t, past(pv_done, u - 2), signal="prob_t_dve")
                pt_done[u] = t

            def weigh_values(u):
                b, half = units[u]
                for slot, head, blk, row, k, place in heads(half):
                    if layer == 0:
                        dst = banks[:, O_BANK[k], place * DV1:(place + 1) * DV1]
                        old = past(norm_done, b - 1, first=state["o_free"])
                    else:
                        dst = banks[:, O_BANK[b % 2], head * DV1:(head + 1) * DV1]
                        old = past(norm_done, b - 2, first=state["o_free"])
                    t = pe.run(lambda e, dst=dst, slot=slot, head=head: e.matmul(
                        dst, prob_t[:, u % 2, slot, :], v_sb[:, b % 2, head, :], start=True, stop=True),
                        pt_copied[u, 0], pt_copied[u, 1], v_ready[b], old,
                        signal="pv" if (slot % 4, k) == (3, 1) else None)
                pv_done[u] = t
                if half < HALVES - 1:
                    return
                s = b % 2
                if layer == 0:
                    o_view = banks[:, O_BANK[0]:O_BANK[1] + 1, 0:4 * DV1].rearrange("p k (s d) -> p k s d", d=DV1)
                    inv = inv_sum[:, s, 0:UH].rearrange("p (k s) -> p k s", k=2)
                    dst = o_sb[:, s, :].rearrange("p (s k d) -> p k s d", k=2, d=DK)
                    t = dve.run(lambda e: e.reciprocal(inv, o_view[:, :, :, DK]), t, signal="inv_sum")
                    t = dve.run(lambda e: e.tensor_tensor(
                        dst, o_view[:, :, :, 0:DK], inv.unsqueeze(3).to_broadcast([P, 2, 4, DK]), ALU.mult), t,
                        past(ot_read, b - 2), signal="o_norm")
                else:
                    o_view = banks[:, O_BANK[s], 0:NH * DV1].rearrange("p (h d) -> p h d", d=DV1)
                    inv = inv_sum[:, s, :]
                    dst = o_sb[:, s, 0:D].rearrange("p (h d) -> p h d", d=DK)
                    t = dve.run(lambda e: e.reciprocal(inv, o_view[:, :, DK]), t, signal="inv_sum")
                    t = dve.run(lambda e: e.tensor_tensor(
                        dst, o_view[:, :, 0:DK], inv.unsqueeze(2).to_broadcast([P, NH, DK]), ALU.mult), t,
                        past(ot_read, b - 2), signal="o_norm")
                norm_done[b] = t

            def transpose_o(b):
                n, free = gen_bank()
                for blk in range(nblk_o):
                    t = pe.run(lambda e, blk=blk: e.transpose(banks[:, n, blk * P:(blk + 1) * P],
                                                              o_sb[:, b % 2, blk * P:(blk + 1) * P], ident[:, :]),
                               norm_done[b], free, signal="o_transposed" if blk == nblk_o - 1 else None)
                ot_read[b] = t
                t = act.run(lambda e: e.activation(
                    o_t[:, b % 2, 0:nblk_o, :].rearrange("p s n -> p (s n)"), banks[:, n, 0:nblk_o * P], ACT.Copy),
                    t, past(y_done, b - 2), signal="o_t")
                gen_free[n] = t
                ot_ready[b] = t
                x_ready[b] = pool.run(lambda e: e.tensor_tensor(x_res[:, b, :], x_res[:, b, :], bo[layer][:, :],
                                                                ALU.add), x_read[b], t_bo[layer], signal="x_bias")

            def project_o(b):
                n, free = gen_bank()
                for blk in range(nblk_o):
                    t = pe.run(lambda e, blk=blk: e.matmul(banks[:, n, 0:D], o_t[:, b % 2, blk, :],
                                                           wo[layer][:, blk, :], start=blk == 0,
                                                           stop=blk == nblk_o - 1),
                               ot_ready[b], free, t_wo[layer], signal="y" if blk == nblk_o - 1 else None)
                y_done[b] = t
                t = dve.run(lambda e: e.scalar_tensor_tensor(
                    x_res[:, b, :], banks[:, n, 0:D], gates[:, layer:layer + 1], x_res[:, b, :],
                    ALU.mult, ALU.add), t, x_ready[b], t_g0, signal="x_attn")
                gen_free[n] = t
                x_ready[b] = t

            def prepare(g):
                yield lambda: slot_of.__setitem__(g, layernorm_group(g))
                for blk in range(4):
                    yield lambda blk=blk: k_block(g, blk)
                for blk in range(4):
                    yield lambda blk=blk: q_block(g, blk)

            def steps():
                for task in prepare(0):
                    task()
                    yield
                per = GS * HALVES
                U = len(units)
                pending = []
                for u in range(U + 4):
                    if u < U:
                        b, half = units[u]
                        if u % per == 0 and b // GS + 1 < NG:
                            pending = list(prepare(b // GS + 1))
                        score(u)
                        left = per - u % per
                    if 0 <= u - 2 < U:
                        weigh_values(u - 2)
                    if u < U and half == 0:
                        v_proj(b)
                    if 0 <= u - 1 < U:
                        transpose_prob(u - 1)
                    if u < U:
                        for _ in range(-(-len(pending) // left)):
                            pending.pop(0)()
                    if u - 3 >= 0 and u - 3 < U and units[u - 3][1] == HALVES - 1:
                        transpose_o(units[u - 3][0])
                    if u - 4 >= 0 and units[u - 4][1] == HALVES - 1:
                        project_o(units[u - 4][0])
                    yield
                state["q_free"] = scores_done[U - 1]
                state["s_free"] = sub_done[U - 1]
                state["pt_free"] = (pt_copied[U - 1, 0], pt_copied[U - 1, 1])
                state["o_free"] = norm_done[NSEQ - 1]

            return steps()

        UP_BANK = (0, 1, 2, 3)
        Y_BANK = (4, 5)

        def moe(layer, banks_free):
            func = (ACT.Silu, ACT.Gelu)[layer]
            up_free = {n: banks_free for n in UP_BANK}
            y_free = {n: banks_free for n in Y_BANK}
            gate = gates[:, 2 + layer:3 + layer]
            hidden_read = {}
            acted_read = {}
            ew_ready, ewt_read = {}, {}
            slot_of = {}
            up_last_read = None
            t_down_done = {}
            acc_done = {}

            def route(g):
                s = slot_of[g]
                n, free = gen_bank()
                for j in range(GS):
                    th, tl = xt_h[:, s, j * P:(j + 1) * P], xt_l[:, s, j * P:(j + 1) * P]
                    t = three_pass(banks[:, n, j * NEXP:(j + 1) * NEXP], th, tl, router_h[layer][:, :],
                                   router_l[layer][:, :], (free, *xt_ready[s], t_small["router", layer]), "router")
                sc, rk = scores[:, s, :, :], ranked[:, s, :, :]
                lg = banks[:, n, 0:GS * NEXP].rearrange("p (j e) -> p j e", e=NEXP)
                old = past(acc_done, g - 2)
                if layer == 0:
                    bias3 = lambda v: v[:, :].unsqueeze(1).to_broadcast([P, GS, NEXP])
                    t = dve.run(lambda e: e.tensor_tensor(sc, lg, bias3(router_b), ALU.add), t, t_small["bias"], old,
                                signal="route")
                    gen_free[n] = t
                    t = dve.run(lambda e: e.tensor_tensor(rk, sc, bias3(select_b), ALU.add), t, signal="route")
                else:
                    t = dve.run(lambda e: e.tensor_copy(sc, lg), t, old, signal="route")
                    gen_free[n] = t
                    rk = sc
                for j in range(GS):
                    t = dve.run(lambda e, j=j: e.max(top_val[:, s, j, :], rk[:, j, :]), t, signal="route")
                for j in range(GS):
                    t = dve.run(lambda e, j=j: e.max_index(top_idx[:, s, j, :], top_val[:, s, j, :], rk[:, j, :]),
                                t, signal="route")
                t = dve.run(lambda e: e.tensor_copy(top_idf[:, s, :, :], top_idx[:, s, :, 0:2]), t, signal="route")
                iota3 = iota8[:, :].unsqueeze(1).to_broadcast([P, GS, NEXP])
                for k, hot in ((0, hot1), (1, hot2)):
                    t = dve.run(lambda e, k=k, hot=hot: e.tensor_tensor(
                        hot[:, s, :, :], iota3, top_idf[:, s, :, k:k + 1].to_broadcast([P, GS, NEXP]),
                        ALU.is_equal), t, t_const, signal="route")
                hd, hs = hot_d[:, s, :, :], hot_s[:, s, :, :]
                t = pool.run(lambda e: e.tensor_tensor(hd, hot1[:, s, :, :], hot2[:, s, :, :], ALU.subtract), t,
                             signal="route_pool")
                t = pool.run(lambda e: e.tensor_tensor(hs, hd, sc, ALU.mult), t, signal="route_pool")
                t = dve.run(lambda e: e.tensor_reduce(lead[:, s, :], hs, AX.X, ALU.add), t, signal="route")
                t = act.run(lambda e: e.activation(lead_w[:, s, :], lead[:, s, :], ACT.Tanh, scale=0.5), t,
                            signal="route_act")
                t = pool.run(lambda e: e.tensor_scalar(lead_w[:, s, :], lead_w[:, s, :], 0.5, 0.5, ALU.mult,
                                                       ALU.add), t, signal="route_pool")
                t = pool.run(lambda e: e.tensor_tensor(
                    hs, hd, lead_w[:, s, :].unsqueeze(2).to_broadcast([P, GS, NEXP]), ALU.mult), t,
                    signal="route_pool")
                t = pool.run(lambda e: e.tensor_tensor(hs, hs, hot2[:, s, :, :], ALU.add), t, signal="route_pool")
                t = pool.run(lambda e: e.tensor_scalar(ew[:, s, :, 0:NEXP], hs, gate, None, ALU.mult), t, old,
                             past(ewt_read, g - 2) if layer == 0 else None, signal="route_pool")
                ew_ready[g] = t

            def down_biases(g):
                s = slot_of[g]
                n, free = gen_bank()
                t = pe.run(lambda e: e.transpose(banks[:, n, 0:P], ew[:, s, :, :].rearrange("p j e -> p (j e)"),
                                                 ident[:, :]), ew_ready[g], free, signal="ew_transposed")
                ewt_read[g] = t
                t = act.run(lambda e: e.activation(ew_t[:, s, :], banks[:, n, 0:P], ACT.Copy), t, signal="ew_t")
                gen_free[n] = t
                m, free = gen_bank()
                for j in range(GS):
                    t = pe.run(lambda e, j=j: e.matmul(
                        banks[:, m, j * D:(j + 1) * D], ew_t[32 * j:32 * j + NEXP, s, :],
                        down_bias[32 * j:32 * j + NEXP, :], start=True, stop=True, tile_position=(32 * j, 0)),
                        t, free, t_small["bias"], signal="down_bias")
                xv = x_res[:, g * GS:(g + 1) * GS, :]
                t = dve.run(lambda e: e.tensor_tensor(
                    xv, banks[:, m, :].rearrange("p (j d) -> p j d", d=D), xv, ALU.add), t,
                    *[x_read[g * GS + j] for j in range(GS)], *[x_ready[g * GS + j] for j in range(GS)],
                    signal="x_down_bias")
                gen_free[m] = t
                for j in range(GS):
                    x_ready[g * GS + j] = t

            def up(g, e8):
                nonlocal up_last_read
                s = slot_of[g]
                h = e8 % 2
                last = g == NG - 1 and False
                tiles = ((0, 2), (1, 3)) if layer == 0 else ((0,), (1,))
                for half, cols in enumerate(tiles):
                    done = {}
                    for c in cols:
                        n = UP_BANK[c] if layer == 0 else UP_BANK[2 * (e8 % 2) + c]
                        done[c] = n, three_pass(
                            banks[:, n, :], up_h[:, e8, c * P:(c + 1) * P], up_l[:, e8, c * P:(c + 1) * P],
                            xt_h[:, s, :], xt_l[:, s, :], (*up_free[n], *xt_ready[s], t_up[layer, e8]), "up")
                        up_last_read = done[c][1]
                    n, t = done[cols[0]]
                    if layer == 0:
                        t = act.run(lambda e, n=n, half=half: e.activation(
                            acted[:, h, half, :], banks[:, n, :], func, bias=up_bias[:, e8, half:half + 1]), t,
                            acted_read.get((h, half)), t_small["bias"], signal="acted")
                        up_free[n] = (t,)
                        nb, tb = done[cols[1]]
                        t = dve.run(lambda e, nb=nb, half=half: e.scalar_tensor_tensor(
                            hidden[:, h, half, :], banks[:, nb, :], up_bias[:, e8, 2 + half:3 + half],
                            acted[:, h, half, :], ALU.add, ALU.mult), tb, t, hidden_read.get(h), signal="hidden")
                        acted_read[h, half] = t
                        up_free[nb] = (t,)
                    else:
                        t = act.run(lambda e, n=n, half=half: e.activation(hidden[:, h, half, :], banks[:, n, :],
                                                                           func), t, hidden_read.get(h),
                                    signal="hidden_act")
                        up_free[n] = (t,)
                    hidden_ready[g, e8, half] = t
                if e8 == NEXP - 1:
                    xt_done[s] = up_last_read

            hidden_ready = {}
            y_turn = [0]

            def down_proj(g, e8):
                s = slot_of[g]
                h = e8 % 2
                n = Y_BANK[y_turn[0] % 2]
                y_turn[0] += 1
                for j in range(GS):
                    for half in (0, 1):
                        t = pe.run(lambda e, j=j, half=half: e.matmul(
                            banks[:, n, j * D:(j + 1) * D], hidden[:, h, half, j * P:(j + 1) * P],
                            down[layer][:, e8, half, :], start=half == 0, stop=half == 1),
                            hidden_ready[g, e8, 0], hidden_ready[g, e8, 1], *y_free[n], t_small["down", layer],
                            signal="y_expert" if (j, half) == (GS - 1, 1) else None)
                hidden_read[h] = t
                for j in range(GS):
                    b = g * GS + j
                    x_ready[b] = dve.run(lambda e, j=j, b=b: e.scalar_tensor_tensor(
                        x_res[:, b, :], banks[:, n, j * D:(j + 1) * D], ew[:, s, j, e8:e8 + 1], x_res[:, b, :],
                        ALU.mult, ALU.add), t, ew_ready[g], x_ready[b], x_read[b], signal="x_moe")
                y_free[n] = (x_ready[g * GS + GS - 1],)
                acc_done[g] = x_ready[g * GS + GS - 1]

            def norm(g):
                slot_of[g] = layernorm_group(g)

            def steps():
                norm(0)
                route(0)
                yield
                order = [(g, e8) for g in range(NG) for e8 in range(NEXP)]
                for i, (g, e8) in enumerate(order):
                    up(g, e8)
                    if i:
                        down_proj(*order[i - 1])
                        if order[i - 1][1] == NEXP - 1:
                            finish(order[i - 1][0])
                    if e8 == 1 and layer == 0:
                        down_biases(g)
                    if e8 == 3 and g + 1 < NG:
                        norm(g + 1)
                    if e8 == 5 and g + 1 < NG:
                        route(g + 1)
                    yield
                down_proj(*order[-1])
                finish(NG - 1)

            def finish(g):
                if layer == 0:
                    return
                t_out.append(sync.run(lambda e: e.dma_start(
                    out.rearrange("b p d -> p b d")[:, g * GS:(g + 1) * GS, :], x_res[:, g * GS:(g + 1) * GS, :]),
                    *[x_ready[g * GS + j] for j in range(GS)], signal="out", by=16))

            def free_tickets():
                return tuple(t for v in (*up_free.values(), *y_free.values()) for t in v), up_last_read

            return steps(), free_tickets

        t_out = []

        def drive(steps):
            for _ in steps:
                pass

        state = {"q_free": t_ctx_all_transposed, "s_free": None, "pt_free": (None, None), "o_free": None}

        def att(layer):
            drive(attention(layer, state))
            pt = state["pt_free"]
            return (state["s_free"], *pt, state["o_free"])

        load_experts(0, ())
        split_layer1_attention_weights()
        free = att(0)
        m0, m0_free = moe(0, free)
        drive(m0)
        free, up_read = m0_free()
        pe.wait(*free)
        state.update(s_free=None, pt_free=(None, None), o_free=None)
        load_experts(1, (up_read,))
        free = att(1)
        m1, m1_free = moe(1, free)
        drive(m1)
        sync.wait(t_out[-1])

        block = stack.enter_context(nc.Block())

        @block.sync
        def _(eng):
            sync.play(eng)

        @block.tensor
        def _(eng):
            pe.play(eng)

        @block.scalar
        def _(eng):
            act.play(eng)

        @block.vector
        def _(eng):
            dve.play(eng)

        @block.gpsimd
        def _(eng):
            pool.play(eng)


_INS = ["x", "ctx_1024", "g_xattn", "g_ffn",
        "L0_xattn_Wq", "L0_xattn_Wk", "L0_xattn_Wv", "L0_xattn_Wo", "L0_xattn_bo",
        "L0_ffn_Wr", "L0_ffn_br", "L0_ffn_Wl1", "L0_ffn_bl1", "L0_ffn_Wl2", "L0_ffn_bl2", "L0_ffn_biases_N",
        "L1_xattn_Wq", "L1_xattn_bq", "L1_xattn_Wk", "L1_xattn_bk", "L1_xattn_Wv", "L1_xattn_bv",
        "L1_xattn_Wo", "L1_xattn_bo", "L1_ffn_router_w", "L1_ffn_w1", "L1_ffn_w2"]


def kernel(**inputs):
    import numpy as _np
    import concourse.bacc as _bacc
    from concourse import mybir as _mybir
    from concourse.bass_utils import run_bass_kernel_spmd as _run

    nc = _bacc.Bacc("TRN2", target_bir_lowering=False, num_devices=1)
    arrays, args = {}, {}
    for name in _INS:
        arr = _np.ascontiguousarray(inputs[name])
        arrays[f"in_{name}_dram"] = arr
        args[name] = nc.dram_tensor(f"in_{name}_dram", arr.shape, _mybir.dt.from_np(arr.dtype),
                                    kind="ExternalInput").ap()
    shape = arrays["in_x_dram"].shape
    out = nc.dram_tensor("out_0_dram", shape, _mybir.dt.float32, kind="ExternalOutput").ap()
    flamingo_two_layers(nc, args, out)
    r = _run(nc, [arrays], core_ids=[0])
    return r.results[0]["out_0_dram"]
```

```python
from contextlib import ExitStack

import concourse.bass as bass
from concourse import mybir

ALU = mybir.AluOpType
ACT = mybir.ActivationFunctionType
AX = mybir.AxisListType
F32 = mybir.dt.float32
F32R = mybir.dt.float32r
U32 = mybir.dt.uint32

P = 128
EPS = 1e-5
PSUM_BANK = 512
PSUM_BANKS = 8


class Lane:

    def __init__(self, name, counts, semaphore):
        self.name, self.counts, self.semaphore = name, counts, semaphore
        self.steps, self.waited = [], {}

    def wait(self, *tickets):
        for ticket in tickets:
            if ticket is not None and self.waited.get(ticket[0], 0) < ticket[1]:
                self.waited[ticket[0]] = ticket[1]
                self.steps.append(("wait", *ticket, 0))

    def run(self, emit, *tickets, signal=None, by=1):
        self.wait(*tickets)
        self.steps.append(("do", emit, signal, by))
        if signal is None:
            return None
        self.semaphore(signal)
        self.counts[signal] = self.counts.get(signal, 0) + by
        return signal, self.counts[signal]

    def play(self, eng):
        for kind, what, arg, by in self.steps:
            if kind == "wait":
                eng.wait_ge(self.semaphore(what), arg)
            else:
                ins = what(eng)
                if arg is not None:
                    ins.then_inc(self.semaphore(arg), by)


def flamingo_two_layers(nc, a, out):
    x_dram, ctx_dram = a["x"], a["ctx_1024"]
    NSEQ, SEQ, D = x_dram.shape
    _, NKEY, _ = ctx_dram.shape
    INNER0 = a["L0_xattn_Wq"].shape[1]
    NEXP, _, TWOH0 = a["L0_ffn_Wl1"].shape
    HID1 = a["L1_ffn_w1"].shape[2]
    DK0, DK1 = 64, 8
    NH0, NH1 = INNER0 // DK0, D // DK1
    GS = 4
    NG = NSEQ // GS
    GT = GS * SEQ
    GK = GS * NKEY
    CTX_ROWS = NSEQ * NKEY
    CTX_BLOCKS = (CTX_ROWS + P - 1) // P
    ROW1 = 32
    UH = 8
    V1_WINDOW = 12
    assert SEQ == P and D == P and GT == PSUM_BANK and NH0 == UH and NH1 == 2 * UH
    assert TWOH0 == 4 * P and HID1 == 2 * P and NEXP == 8

    with ExitStack() as stack:
        def sbuf(name, shape, dt=F32):
            return stack.enter_context(nc.sbuf_tensor(name, shape, dt))

        semaphores = {}

        def semaphore(name):
            if name not in semaphores:
                semaphores[name] = stack.enter_context(nc.semaphore(name))
            return semaphores[name]

        counts = {}
        sync = Lane("sync", counts, semaphore)
        pe = Lane("pe", counts, semaphore)
        act = Lane("act", counts, semaphore)
        dve = Lane("dve", counts, semaphore)
        pool = Lane("pool", counts, semaphore)

        def load(lane, dst, src, name, scattered=False):
            return lane.run(lambda e: e.dma_start(dst, src, allow_slow_non_contiguous=scattered),
                            signal="in_" + name, by=16)

        x_res = sbuf("x_res", [P, NSEQ, D])
        ident = sbuf("ident", [P, P])
        iota8 = sbuf("iota8", [P, NEXP])
        head_mask = sbuf("head_mask", [P, 4])
        gates_raw = sbuf("gates_raw", [P, 4])
        gates = sbuf("gates", [P, 4])
        minus_half = sbuf("minus_half", [P, GS])
        ctx_th = sbuf("ctx_th", [P, CTX_ROWS], F32R)
        ctx_tl = sbuf("ctx_tl", [P, CTX_ROWS], F32R)

        BLOCKS = (INNER0 // P, 1)
        wq_h = [sbuf(f"wq{l}_h", [P, BLOCKS[l], P], F32R) for l in (0, 1)]
        wq_l = [sbuf(f"wq{l}_l", [P, BLOCKS[l], P], F32R) for l in (0, 1)]
        wk_h = [sbuf(f"wk{l}_h", [P, BLOCKS[l], P], F32R) for l in (0, 1)]
        wk_l = [sbuf(f"wk{l}_l", [P, BLOCKS[l], P], F32R) for l in (0, 1)]
        wv0_h = sbuf("wv0_h", [P, INNER0], F32R)
        wv0_l = sbuf("wv0_l", [P, INNER0], F32R)
        wv1 = sbuf("wv1", [P, D])
        wo = [sbuf("wo0", [P, 4, D]), sbuf("wo1", [P, 1, D])]
        bq1 = sbuf("bq1", [P, 1])
        bk1 = sbuf("bk1", [P, 1])
        bv1 = sbuf("bv1", [NKEY, D])
        bo = [sbuf("bo0", [P, D]), sbuf("bo1", [P, D])]

        up_h = sbuf("up_h", [P, NEXP, TWOH0], F32R)
        up_l = sbuf("up_l", [P, NEXP, TWOH0], F32R)
        down = [sbuf("down0", [P, NEXP, 2, D]), sbuf("down1", [P, NEXP, 2, D])]
        up_bias = sbuf("up_bias", [P, NEXP, 4])
        down_bias = sbuf("down_bias", [P, GS, D])
        router = [sbuf(f"router{l}", [P, NEXP]) for l in (0, 1)]
        router_h = [sbuf(f"router{l}_h", [P, NEXP], F32R) for l in (0, 1)]
        router_l = [sbuf(f"router{l}_l", [P, NEXP], F32R) for l in (0, 1)]
        router_b = sbuf("router_b", [P, NEXP])
        select_b = sbuf("select_b", [P, NEXP])

        stats = sbuf("stats", [P, 2, GS, 6])
        mean_var = sbuf("mean_var", [P, 2, GS, 2])
        rstd = sbuf("rstd", [P, 2, GS])
        x_norm = sbuf("x_norm", [P, 2, GS, D])
        xt_h = sbuf("xt_h", [P, 2, GT], F32R)
        xt_l = sbuf("xt_l", [P, 2, GT], F32R)

        v0 = sbuf("v0", [NKEY, 2, NH0, DK0 + 1])
        v1 = sbuf("v1", [NKEY, 2, NH1 + V1_WINDOW - 1, DK1 + 1])
        prob = sbuf("prob", [P, 2, UH, NKEY])
        prob_t = sbuf("prob_t", [NKEY, 2, UH, SEQ])
        row_max = sbuf("row_max", [P, 2, UH])
        inv_sum = sbuf("inv_sum", [P, 2, NH1])
        o_sb = sbuf("o_sb", [P, 2, INNER0])
        o_t = sbuf("o_t", [P, 2, 4, SEQ])

        scores = sbuf("scores", [P, 2, GS, NEXP])
        ranked = sbuf("ranked", [P, 2, GS, NEXP])
        top_val = sbuf("top_val", [P, 2, GS, 8])
        top_idx = sbuf("top_idx", [P, 2, GS, 8], U32)
        top_idf = sbuf("top_idf", [P, 2, GS, 2])
        hot1 = sbuf("hot1", [P, 2, GS, NEXP])
        hot2 = sbuf("hot2", [P, 2, GS, NEXP])
        hot_d = sbuf("hot_d", [P, 2, GS, NEXP])
        hot_s = sbuf("hot_s", [P, 2, GS, NEXP])
        lead = sbuf("lead", [P, 2, GS])
        lead_w = sbuf("lead_w", [P, 2, GS])
        ew = sbuf("ew", [P, 2, GS, 32])
        ew_t = sbuf("ew_t", [P, 2, P])
        acted = sbuf("acted", [P, 2, 2, GT])
        hidden = sbuf("hidden", [P, 2, 2, GT])
        up_raw = sbuf("up_raw", [P, 2, TWOH0])

        layer0_only = ExitStack()
        q0_t = layer0_only.enter_context(nc.sbuf_tensor("q0_t", [P, 2, 4, GT], F32))
        k0_diag = layer0_only.enter_context(nc.sbuf_tensor("k0_diag", [P, 2, 4, GS, 2, NKEY], F32))
        layer0_only.close()
        q1_t = sbuf("q1_t", [P, 2, 2, GT], F32R)
        k1_t = sbuf("k1_t", [P, 2, 2, GK], F32R)
        k1_diag = sbuf("k1_diag", [P, 2, 2, GS, 4, NKEY], F32R)

        banks = stack.enter_context(nc.psum_tensor("banks", [P, PSUM_BANKS, PSUM_BANK], F32))

        def past(tickets, n, *rest, first=None):
            return first if n < 0 else tickets[(n, *rest) if rest else n]

        def split_weight(lane, name, stage, hi, lo, *after):
            th = lane.run(lambda e: e.tensor_copy(hi, stage), *after, signal=name + "_hi")
            return lane.run(lambda e: e.tensor_tensor(lo, stage, hi.bitcast(F32), ALU.subtract), th,
                            signal=name + "_lo")

        raw = [view[:, i, j, :] for view in (acted, hidden) for i in (0, 1) for j in (0, 1)]
        t_ctx = []
        ctx_flat = ctx_dram.rearrange("b k d -> (b k) d")
        full_blocks = CTX_ROWS // P
        ctx_stage = q0_t[:, :, :, :].rearrange("p a b c -> p (a b c)").rearrange("p (n d) -> p n d", d=D)
        t_x = []
        xg = x_dram.rearrange("b p d -> p b d")
        t_x.append(load(sync, x_res[:, 0:GS, :], xg[:, 0:GS, :], "x0"))
        t_ctx_full = load(act, ctx_stage[:, 0:full_blocks, :],
                          ctx_flat[0:full_blocks * P, :].rearrange("(n p) d -> p n d", p=P), "ctx")
        tail = CTX_ROWS - full_blocks * P
        t_ctx_tail = load(act, ctx_stage[0:tail, full_blocks, :], ctx_flat[full_blocks * P:, :], "ctx_tail")
        raw_w = {}
        t_raw = {}
        for slot, (name, src) in enumerate((("wq0", a["L0_xattn_Wq"]), ("wk0", a["L0_xattn_Wk"]),
                                            ("wv0", a["L0_xattn_Wv"]))):
            raw_w[name] = raw[slot]
            t_raw[name] = load(sync, raw_w[name], src, name)
        t_gates_x = load(sync, gates_raw[:, 0:2], a["g_xattn"].partition_broadcast(P), "g_xattn")
        t_gates_f = load(sync, gates_raw[:, 2:4], a["g_ffn"].partition_broadcast(P), "g_ffn")
        t_bo = [load(sync, bo[l][:, :], a[f"L{l}_xattn_bo"].partition_broadcast(P), f"bo{l}") for l in (0, 1)]
        t_wo = [load(sync, wo[l][:, :, :], a[f"L{l}_xattn_Wo"].rearrange("(t p) n -> p t n", p=P), f"wo{l}")
                for l in (0, 1)]
        for g in range(1, NG):
            t_x.append(load(sync, x_res[:, g * GS:(g + 1) * GS, :], xg[:, g * GS:(g + 1) * GS, :], f"x{g}"))
        for slot, name in ((3, "Wq"), (4, "Wk")):
            key = name.lower() + "1"
            raw_w[key] = raw[slot][:, 0:D]
            t_raw[key] = load(sync, raw_w[key], a[f"L1_xattn_{name}"], key)
        t_wv1 = load(sync, wv1[:, :], a["L1_xattn_Wv"], "wv1")
        t_bv1 = load(sync, bv1[:, :], a["L1_xattn_bv"].partition_broadcast(NKEY), "bv1")

        t_ident0 = pool.run(lambda e: e.memset(ident[:, :], 0.0), signal="ident")
        t_ident = pool.run(lambda e: e.affine_select(
            out=ident[:, :], in_=ident[:, :], compare_op=ALU.not_equal, fill=1.0, base=0,
            pattern=[[-1, P]], channel_multiplier=1), t_ident0, signal="ident")
        t_mhalf = pool.run(lambda e: e.memset(minus_half[:, :], -0.5), signal="constants")
        t_const = t_mhalf
        for e8 in range(NEXP):
            t_const = pool.run(lambda e, e8=e8: e.memset(iota8[:, e8:e8 + 1], float(e8)), signal="constants")
        for t in (v0[:, :, :, DK0:], v1[:, :, :, :]):
            t_const = pool.run(lambda e, t=t: e.memset(t, 1.0), signal="constants")
        hm = head_mask[:, :]
        t_mask = pool.run(lambda e: e.memset(hm, 1.0), signal="head_mask")
        for i in range(4):
            q = head_mask[ROW1 * i:ROW1 * (i + 1), :]
            t_q = pool.run(lambda e, q=q: e.affine_select(
                out=q, in_=q, compare_op=ALU.is_ge, fill=0.0, base=0, pattern=[[-DK1, 4]], channel_multiplier=1),
                t_mask, signal="head_mask_part")
            t_mask_last = pool.run(lambda e, q=q: e.affine_select(
                out=q, in_=q, compare_op=ALU.is_ge, fill=0.0, base=DK1 - 1, pattern=[[DK1, 4]],
                channel_multiplier=-1), t_q, signal="head_mask_part")
        t_mask = t_mask_last
        t_const = pool.run(lambda e: e.memset(ew[:, :, :, :], 0.0), t_mask, signal="constants")
        load(sync, bq1[:, :], a["L1_xattn_bq"].rearrange("(p o) -> p o", o=1), "bqk1", scattered=True)
        t_bqk1 = load(sync, bk1[:, :], a["L1_xattn_bk"].rearrange("(p o) -> p o", o=1), "bqk1", scattered=True)
        t_db_zero = pool.run(lambda e: e.memset(down_bias[:, :, :], 0.0), signal="constants")
        t_k0_zero = pool.run(lambda e: e.memset(k0_diag[:, :, :, :, :, :], 0.0), signal="k0_zero")

        t_g0 = act.run(lambda e: e.activation(gates[:, :], gates_raw[:, :], ACT.Tanh), t_gates_x, t_gates_f,
                       signal="gates")
        t_bo_g = [pool.run(lambda e, l=l: e.tensor_scalar(bo[l][:, :], bo[l][:, :], gates[:, l:l + 1], None,
                                                          ALU.mult), t_g0, t_bo[l], signal="bo_gated")
                  for l in (0, 1)]

        GEN = (6, 7)
        gen_free = {6: None, 7: None}
        gen_turn = [0]

        def gen_bank():
            n = GEN[gen_turn[0] % 2]
            gen_turn[0] += 1
            return n, gen_free[n]

        t_ctx_t = []
        for first in range(0, CTX_BLOCKS, 4):
            n, free = gen_bank()
            last = min(first + 4, CTX_BLOCKS)
            for j in range(first, last):
                rows = min(P, CTX_ROWS - j * P)
                t = pe.run(lambda e, j=j, rows=rows, n=n, first=first: e.transpose(
                    banks[:, n, (j - first) * P:(j - first) * P + rows], ctx_stage[0:rows, j, :],
                    ident[0:rows, 0:rows]), free, t_ident, t_ctx_full, t_ctx_tail,
                    signal="ctx_transposed" if j == last - 1 else None)
            c0, c1 = first * P, min(last * P, CTX_ROWS)
            th = act.run(lambda e, n=n, c0=c0, c1=c1: e.activation(ctx_th[:, c0:c1], banks[:, n, 0:c1 - c0],
                                                                   ACT.Copy), t, signal="ctx_th")
            tl = dve.run(lambda e, n=n, c0=c0, c1=c1: e.tensor_tensor(
                ctx_tl[:, c0:c1], banks[:, n, 0:c1 - c0], ctx_th[:, c0:c1].bitcast(F32), ALU.subtract), th,
                signal="ctx_tl")
            gen_free[n] = tl
            t_ctx_t.append(tl)
        t_ctx_all_transposed = t

        def ctx_ready(row_end):
            return t_ctx_t[min((row_end - 1) // (4 * P), len(t_ctx_t) - 1)]

        t_w = {}
        for name, hi, lo, lane in (("wq0", wq_h[0], wq_l[0], pool), ("wk0", wk_h[0], wk_l[0], dve)):
            t_w[name] = split_weight(lane, name, raw_w[name].rearrange("p (a b) -> p a b", a=4),
                                     hi[:, :, :], lo[:, :, :], t_raw[name])
        t_w["wv0"] = split_weight(dve, "wv0", raw_w["wv0"], wv0_h[:, :], wv0_l[:, :], t_raw["wv0"])

        def split_layer1_attention_weights():
            for name, hi, lo in (("wq1", wq_h[1], wq_l[1]), ("wk1", wk_h[1], wk_l[1])):
                t_w[name] = split_weight(pool, name, raw_w[name], hi[:, 0, :], lo[:, 0, :], t_raw[name])

        up_raw_free = {}
        t_up = {}
        t_small = {}

        def load_experts(layer, after):
            width = TWOH0 if layer == 0 else HID1
            src_up = a["L0_ffn_Wl1"] if layer == 0 else a["L1_ffn_w1"]
            src_down = a["L0_ffn_Wl2"] if layer == 0 else a["L1_ffn_w2"]
            t_small["down", layer] = load(sync, down[layer][:, :, :, :],
                                          src_down.rearrange("e (t p) d -> p e t d", p=P), f"down{layer}")
            src_router = a["L0_ffn_Wr"] if layer == 0 else a["L1_ffn_router_w"]
            t_r = load(sync, router[layer][:, :], src_router.rearrange("n d -> d n"), f"router{layer}",
                       scattered=True)
            t_small["router", layer] = split_weight(pool, f"router{layer}", router[layer][:, :],
                                                    router_h[layer][:, :], router_l[layer][:, :], t_r)
            if layer == 0:
                load(sync, up_bias[:, :, :], a["L0_ffn_bl1"].rearrange("e (t p) -> p e t", p=P), "moe_bias",
                     scattered=True)
                for i in range(4):
                    sync.wait(t_db_zero)
                    load(sync, down_bias[32 * i:32 * i + NEXP, i, :], a["L0_ffn_bl2"], "moe_bias")
                load(sync, router_b[:, :], a["L0_ffn_br"].partition_broadcast(P), "moe_bias")
                t_small["bias"] = load(sync, select_b[:, :], a["L0_ffn_biases_N"].partition_broadcast(P),
                                       "moe_bias")
            for e8 in range(NEXP):
                slot = e8 % 2
                stage = up_raw[:, slot, 0:width]
                first_after = up_raw_free.get(slot)
                t_in = sync.run(lambda e, stage=stage, e8=e8: e.dma_start(stage, src_up[e8]), first_after,
                                *(after if e8 == 0 else ()), signal=f"in_up_slot{slot}", by=16)
                t_up[layer, e8] = split_weight(pool, "up_split", stage, up_h[:, e8, 0:width],
                                               up_l[:, e8, 0:width], t_in, *(after if e8 == 0 else ()))
                up_raw_free[slot] = t_up[layer, e8]


        x_ready = {b: t_x[b // GS] for b in range(NSEQ)}
        x_read = {b: None for b in range(NSEQ)}
        xt_done = {0: None, 1: None}
        xt_ready = {}
        norm_turn = [0]

        def layernorm_group(g):
            s = norm_turn[0] % 2
            norm_turn[0] += 1
            seqs = [g * GS + j for j in range(GS)]
            for j, b in enumerate(seqs):
                t_stats = dve.run(lambda e, b=b, j=j: e.bn_stats(stats[:, s, j, :], x_res[:, b, :]), x_ready[b],
                                  signal="ln_stats")
            for j in range(GS):
                t_mv = dve.run(lambda e, j=j: e.bn_aggr(mean_var[:, s, j, :], stats[:, s, j, :]), t_stats,
                               ln_free[s], signal="ln_mean_var")
            t_eps = pool.run(lambda e: e.tensor_scalar(rstd[:, s, :], mean_var[:, s, :, 1], EPS, None, ALU.add),
                             t_mv, ln_free[s], signal="ln_eps")
            t_rstd = pool.run(lambda e: e.tensor_tensor(rstd[:, s, :], rstd[:, s, :], minus_half[:, :], ALU.pow),
                              t_eps, t_mhalf, signal="ln_rstd")
            norm_ready[s] = t_rstd
            return s

        def normalize(g, s):
            for j in range(GS):
                b = g * GS + j
                t = dve.run(lambda e, b=b, j=j: e.tensor_scalar(
                    x_norm[:, s, j, :], x_res[:, b, :], mean_var[:, s, j, 0:1], rstd[:, s, j:j + 1],
                    ALU.subtract, ALU.mult), norm_ready[s], ln_free[s], x_ready[b], signal="ln_out")
                x_read[b] = t
            norm_ready[s] = t

        def transpose_norm(s):
            t_norm = norm_ready[s]
            n, free = gen_bank()
            for j in range(GS):
                t = pe.run(lambda e, j=j: e.transpose(banks[:, n, j * P:(j + 1) * P], x_norm[:, s, j, :],
                                                      ident[:, :]), t_norm, free, t_ident,
                           signal="ln_transposed" if j == GS - 1 else None)
            ln_free[s] = t
            t_h = act.run(lambda e: e.activation(xt_h[:, s, :], banks[:, n, :], ACT.Copy), t, xt_done[s],
                          signal="xt_h")
            t_l = dve.run(lambda e: e.tensor_tensor(xt_l[:, s, :], banks[:, n, :], xt_h[:, s, :].bitcast(F32),
                                                    ALU.subtract), t_h, xt_done[s], signal="xt_l")
            gen_free[n] = t_l
            xt_ready[s] = (t_h, t_l)

        norm_ready = {}
        ln_free = {0: None, 1: None}

        def three_pass(outp, wh, wl, xh, xl, tickets, signal):
            pe.run(lambda e: e.matmul(outp, wh, xh, start=True, stop=False), *tickets)
            pe.run(lambda e: e.matmul(outp, wl, xh, start=False, stop=False))
            return pe.run(lambda e: e.matmul(outp, wh, xl, start=False, stop=True), signal=signal)

        S_BANK = (0, 1)
        PT_BANK = (2, 3)
        O_BANK = (4, 5)

        def attention(layer, state):
            DK = (DK0, DK1)[layer]
            NH = (NH0, NH1)[layer]
            DV1 = DK + 1
            window = (1, V1_WINDOW)[layer]
            HALVES = NH // UH
            v_sb = (v0, v1)[layer]
            SCALE = float(DK) ** -0.5
            nblk_o = (4, 1)[layer]

            def heads(half):
                for slot in range(UH):
                    yield slot, UH * half + slot, slot // 4, slot % 4

            units = [(b, h) for b in range(NSEQ) for h in range(HALVES)]
            q_ready, k_ready, v_ready = {}, {}, {}
            scores_done = {}
            pv_done, prob_t_read = {}, {}
            sub_done, exp_done, pt_done, pt_copied, norm_done, ot_ready, y_done = {}, {}, {}, {}, {}, {}, {}
            ot_read = {}
            last_unit = lambda b: b * HALVES + HALVES - 1
            slot_of = {}

            def q_block(g, blk):
                s = slot_of[g]
                n, free = gen_bank()
                old = past(scores_done, last_unit(g * GS - GS - 1) if g >= 2 else -1, first=state["q_free"])
                t = three_pass(banks[:, n, :], wq_h[layer][:, blk, :], wq_l[layer][:, blk, :],
                               xt_h[:, s, :], xt_l[:, s, :], (free, *xt_ready[s], t_w[f"wq{layer}"]), "q_proj")
                if blk == nblk_o - 1:
                    xt_done[s] = t
                if layer == 0:
                    t = act.run(lambda e: e.activation(q0_t[:, g % 2, blk, :], banks[:, n, :], ACT.Copy), t, old,
                                signal="q_t")
                else:
                    t = act.run(lambda e: e.activation(q1_t[:, g % 2, 0, :], banks[:, n, :], ACT.Identity,
                                                       bias=bq1[:, 0:1]), t, old, t_bqk1, signal="q_t")
                    t = dve.run(lambda e: e.scalar_tensor_tensor(
                        q1_t[:, g % 2, 1, :], banks[:, n, :], bq1[:, 0:1], q1_t[:, g % 2, 0, :].bitcast(F32),
                        ALU.add, ALU.subtract), t, old, t_bqk1, signal="q_tl")
                gen_free[n] = t
                q_ready[g] = t

            def k_block(g, blk):
                c0 = g * GK
                n, free = gen_bank()
                t = three_pass(banks[:, n, 0:GK], wk_h[layer][:, blk, :], wk_l[layer][:, blk, :],
                               ctx_th[:, c0:c0 + GK], ctx_tl[:, c0:c0 + GK],
                               (free, ctx_ready(c0 + GK), t_w[f"wk{layer}"]), "k_proj")
                if layer == 0:
                    old = past(scores_done, last_unit(g * GS - GS - 1) if g >= 2 else -1, first=t_k0_zero)
                    for k in (0, 1):
                        rows = slice(DK0 * k, DK0 * (k + 1))
                        t = act.run(lambda e, k=k, rows=rows: e.activation(
                            k0_diag[rows, g % 2, blk, :, k, :],
                            banks[rows, n, 0:GK].rearrange("p (j n) -> p j n", n=NKEY), ACT.Copy), t if k == 0 else None,
                            old, signal="k_t")
                    gen_free[n] = t
                else:
                    old = past(k_ready, g - 2, first=state["q_free"])
                    t = act.run(lambda e: e.activation(k1_t[:, g % 2, 0, :], banks[:, n, 0:GK], ACT.Identity,
                                                       bias=bk1[:, 0:1]), t, old, t_bqk1, signal="k_t")
                    t = dve.run(lambda e: e.scalar_tensor_tensor(
                        k1_t[:, g % 2, 1, :], banks[:, n, 0:GK], bk1[:, 0:1], k1_t[:, g % 2, 0, :].bitcast(F32),
                        ALU.add, ALU.subtract), t, old, t_bqk1, signal="k_tl")
                    gen_free[n] = t
                    parts = k1_t[:, g % 2, :, :].bitcast(F32).rearrange("p c (j n) -> p (c j) n", n=NKEY)
                    t = pool.run(lambda e: e.tensor_tensor(
                        k1_diag[:, g % 2, :, :, :, :].rearrange("p c j q n -> p (c j) q n"),
                        parts.unsqueeze(2).to_broadcast([P, 2 * GS, 4, NKEY]),
                        head_mask[:, :].unsqueeze(1).unsqueeze(3).to_broadcast([P, 2 * GS, 4, NKEY]), ALU.mult),
                        t, t_mask, past(scores_done, last_unit(g * GS - GS - 1) if g >= 2 else -1,
                                        first=state["q_free"]), signal="k1_diag")
                k_ready[g] = t

            def v_proj(b):
                c0 = b * NKEY
                n, free = gen_bank()
                old = past(pv_done, last_unit(b - 2) if b >= 2 else -1)
                if layer == 0:
                    t = three_pass(banks[0:NKEY, n, :], ctx_th[:, c0:c0 + NKEY], ctx_tl[:, c0:c0 + NKEY],
                                   wv0_h[:, :], wv0_l[:, :], (free, ctx_ready(c0 + NKEY), t_w["wv0"]), "v_proj")
                    t = dve.run(lambda e: e.tensor_copy(
                        v0[:, b % 2, :, 0:DK0], banks[0:NKEY, n, :].rearrange("p (h d) -> p h d", d=DK0)),
                        t, old, signal="v")
                else:
                    pe.run(lambda e: e.matmul(banks[0:NKEY, n, 0:D], ctx_th[:, c0:c0 + NKEY].bitcast(F32),
                                              wv1[:, :], start=True, stop=False), free, ctx_ready(c0 + NKEY), t_wv1)
                    t = pe.run(lambda e: e.matmul(banks[0:NKEY, n, 0:D], ctx_tl[:, c0:c0 + NKEY].bitcast(F32),
                                                  wv1[:, :], start=False, stop=True), signal="v_proj")
                    t = dve.run(lambda e: e.tensor_tensor(
                        v1[:, b % 2, 0:NH1, 0:DK1], banks[0:NKEY, n, 0:D].rearrange("p (h d) -> p h d", d=DK1),
                        bv1[:, :].rearrange("p (h d) -> p h d", d=DK1), ALU.add), t, old, t_bv1, signal="v")
                gen_free[n] = t
                v_ready[b] = t

            def score(u):
                b, half = units[u]
                g, j = b // GS, b % GS
                tok = slice(j * SEQ, (j + 1) * SEQ)
                free = past(sub_done, u - 1, first=state["s_free"])
                if layer == 0:
                    for blk in range(4):
                        c0 = 2 * (blk % 2) * NKEY
                        t = pe.run(lambda e, blk=blk, c0=c0: e.matmul(
                            banks[:, S_BANK[blk // 2], c0:c0 + 2 * NKEY], q0_t[:, g % 2, blk, tok],
                            k0_diag[:, g % 2, blk, j, :, :].rearrange("p h n -> p (h n)"), start=True, stop=True),
                            q_ready[g], k_ready[g], free, signal="scores" if blk == 3 else None)
                else:
                    passes = [(0, 0, 0), (0, 0, 1), (0, 1, 0), (0, 1, 1), (1, 0, 0), (1, 0, 1)]
                    for i, (q_part, k_part, k) in enumerate(passes):
                        row = ROW1 * (2 * half + k)
                        t = pe.run(lambda e, q_part=q_part, k_part=k_part, k=k, row=row: e.matmul(
                            banks[:, S_BANK[k], 0:4 * NKEY], q1_t[row:row + ROW1, g % 2, q_part, tok],
                            k1_diag[row:row + ROW1, g % 2, k_part, j, :, :].rearrange("p h n -> p (h n)"),
                            start=(q_part, k_part) == (0, 0), stop=q_part == 1, tile_position=(row, 0)),
                            q_ready[g], k_ready[g], free, signal="scores" if i == 5 else None)
                scores_done[u] = t
                s_view = banks[:, S_BANK[0]:S_BANK[1] + 1, 0:4 * NKEY].rearrange("p k (s n) -> p k s n", n=NKEY)
                m_view = row_max[:, u % 2, :].rearrange("p (k s) -> p k s", k=2)
                p_view = prob[:, u % 2, :, :].rearrange("p (k s) n -> p k s n", k=2)
                t = dve.run(lambda e: e.tensor_reduce(m_view, s_view, AX.X, ALU.max), t, signal="row_max")
                t = dve.run(lambda e: e.tensor_tensor(
                    p_view, s_view, m_view.unsqueeze(3).to_broadcast([P, 2, 4, NKEY]), ALU.subtract), t,
                    past(pt_done, u - 2), signal="shifted")
                sub_done[u] = t
                exp_done[u] = act.run(lambda e: e.activation(prob[:, u % 2, :, :], prob[:, u % 2, :, :], ACT.Exp,
                                                             scale=SCALE), t, signal="exp")

            def transpose_prob(u):
                for k in (0, 1):
                    for place in range(4):
                        t = pe.run(lambda e, k=k, place=place: e.transpose(
                            banks[0:NKEY, PT_BANK[k], place * SEQ:(place + 1) * SEQ],
                            prob[:, u % 2, 4 * k + place, :], ident[:, :]),
                            exp_done[u], past(pt_copied, u - 1, k, first=state["pt_free"][k]),
                            signal="prob_transposed" if place == 3 else None)
                    dst = prob_t[:, u % 2, 4 * k:4 * k + 4, :].rearrange("p s n -> p (s n)")
                    if k == 0 or (layer == 1 and u % 2 == 0):
                        pt_copied[u, k] = act.run(lambda e, dst=dst, k=k: e.activation(
                            dst, banks[0:NKEY, PT_BANK[k], :], ACT.Copy), t, past(pv_done, u - 2), signal="prob_t_act")
                    else:
                        pt_copied[u, k] = dve.run(lambda e, dst=dst, k=k: e.tensor_copy(
                            dst, banks[0:NKEY, PT_BANK[k], :]), t, past(pv_done, u - 2), signal="prob_t_dve")
                pt_done[u] = t

            def weigh_values(u):
                b, half = units[u]
                for slot, head, k, place in heads(half):
                    if layer == 0:
                        dst = banks[:, O_BANK[k], place * DV1:(place + 1) * DV1]
                        old = past(norm_done, b - 1, first=state["o_free"])
                    else:
                        dst = banks[:, O_BANK[b % 2], head * DV1:(head + V1_WINDOW) * DV1]
                        old = past(norm_done, b - 2, first=state["o_free"])
                    t = pe.run(lambda e, dst=dst, slot=slot, head=head: e.matmul(
                        dst, prob_t[:, u % 2, slot, :],
                        v_sb[:, b % 2, head:head + window, :].rearrange("p h d -> p (h d)"), start=True, stop=True),
                        pt_copied[u, 0], pt_copied[u, 1], v_ready[b], old,
                        signal="pv" if slot == UH - 1 else None)
                pv_done[u] = t
                if half < HALVES - 1:
                    return
                s = b % 2
                if layer == 0:
                    o_view = banks[:, O_BANK[0]:O_BANK[1] + 1, 0:4 * DV1].rearrange("p k (s d) -> p k s d", d=DV1)
                    inv = inv_sum[:, s, 0:UH].rearrange("p (k s) -> p k s", k=2)
                    dst = o_sb[:, s, :].rearrange("p (k s d) -> p k s d", k=2, d=DK)
                    t = dve.run(lambda e: e.reciprocal(inv, o_view[:, :, :, DK]), t, signal="inv_sum")
                    t = dve.run(lambda e: e.tensor_tensor(
                        dst, o_view[:, :, :, 0:DK], inv.unsqueeze(3).to_broadcast([P, 2, 4, DK]), ALU.mult), t,
                        past(ot_read, b - 2), signal="o_norm")
                else:
                    o_view = banks[:, O_BANK[s], 0:NH * DV1].rearrange("p (h d) -> p h d", d=DV1)
                    inv = inv_sum[:, s, :]
                    dst = o_sb[:, s, 0:D].rearrange("p (h d) -> p h d", d=DK)
                    t = dve.run(lambda e: e.reciprocal(inv, o_view[:, :, DK]), t, signal="inv_sum")
                    t = dve.run(lambda e: e.tensor_tensor(
                        dst, o_view[:, :, 0:DK], inv.unsqueeze(2).to_broadcast([P, NH, DK]), ALU.mult), t,
                        past(ot_read, b - 2), signal="o_norm")
                norm_done[b] = t

            def transpose_o(b):
                n, free = gen_bank()
                for blk in range(nblk_o):
                    t = pe.run(lambda e, blk=blk: e.transpose(banks[:, n, blk * P:(blk + 1) * P],
                                                              o_sb[:, b % 2, blk * P:(blk + 1) * P], ident[:, :]),
                               norm_done[b], free, signal="o_transposed" if blk == nblk_o - 1 else None)
                ot_read[b] = t
                t = act.run(lambda e: e.activation(
                    o_t[:, b % 2, 0:nblk_o, :].rearrange("p s n -> p (s n)"), banks[:, n, 0:nblk_o * P], ACT.Copy),
                    t, past(y_done, b - 2), signal="o_t")
                gen_free[n] = t
                ot_ready[b] = t
                x_ready[b] = pool.run(lambda e: e.tensor_tensor(x_res[:, b, :], x_res[:, b, :], bo[layer][:, :],
                                                                ALU.add), x_read[b], t_bo[layer], signal="x_bias")

            def project_o(b):
                n, free = gen_bank()
                for blk in range(nblk_o):
                    t = pe.run(lambda e, blk=blk: e.matmul(banks[:, n, 0:D], o_t[:, b % 2, blk, :],
                                                           wo[layer][:, blk, :], start=blk == 0,
                                                           stop=blk == nblk_o - 1),
                               ot_ready[b], free, t_wo[layer], signal="y" if blk == nblk_o - 1 else None)
                y_done[b] = t
                t = dve.run(lambda e: e.scalar_tensor_tensor(
                    x_res[:, b, :], banks[:, n, 0:D], gates[:, layer:layer + 1], x_res[:, b, :],
                    ALU.mult, ALU.add), t, x_ready[b], t_g0, signal="x_attn")
                gen_free[n] = t
                x_ready[b] = t

            def prepare(g):
                yield lambda: slot_of.__setitem__(g, layernorm_group(g))
                for blk in range(nblk_o):
                    yield lambda blk=blk: k_block(g, blk)
                    if blk == 0:
                        yield lambda: normalize(g, slot_of[g])
                    if blk == min(1, nblk_o - 1):
                        yield lambda: transpose_norm(slot_of[g])
                for blk in range(nblk_o):
                    yield lambda blk=blk: q_block(g, blk)

            def steps():
                for task in prepare(0):
                    task()
                    yield
                per = GS * HALVES
                U = len(units)
                pending = []
                for u in range(U + 4):
                    if u < U:
                        b, half = units[u]
                        if u % per == 0 and b // GS + 1 < NG:
                            pending = list(prepare(b // GS + 1))
                        score(u)
                        left = per - u % per
                    if 0 <= u - 2 < U:
                        weigh_values(u - 2)
                    if u < U and half == 0:
                        v_proj(b)
                    if 0 <= u - 1 < U:
                        transpose_prob(u - 1)
                    if u < U:
                        for _ in range(-(-len(pending) // left)):
                            pending.pop(0)()
                    if u - 3 >= 0 and u - 3 < U and units[u - 3][1] == HALVES - 1:
                        transpose_o(units[u - 3][0])
                    if u - 4 >= 0 and units[u - 4][1] == HALVES - 1:
                        project_o(units[u - 4][0])
                    yield
                state["q_free"] = scores_done[U - 1]
                state["s_free"] = sub_done[U - 1]
                state["pt_free"] = (pt_copied[U - 1, 0], pt_copied[U - 1, 1])
                state["o_free"] = norm_done[NSEQ - 1]

            return steps()

        UP_BANK = (0, 1, 2, 3)
        Y_BANK = (4, 5)

        def moe(layer, banks_free):
            func = (ACT.Silu, ACT.Gelu)[layer]
            up_free = {n: banks_free for n in UP_BANK}
            y_free = {n: banks_free for n in Y_BANK}
            gate = gates[:, 2 + layer:3 + layer]
            hidden_read = {}
            acted_read = {}
            ew_ready, ewt_read = {}, {}
            slot_of = {}
            up_last_read = None
            t_down_done = {}
            acc_done = {}

            def route(g):
                s = slot_of[g]
                n, free = gen_bank()
                for j in range(GS):
                    th, tl = xt_h[:, s, j * P:(j + 1) * P], xt_l[:, s, j * P:(j + 1) * P]
                    t = three_pass(banks[:, n, j * NEXP:(j + 1) * NEXP], th, tl, router_h[layer][:, :],
                                   router_l[layer][:, :], (free, *xt_ready[s], t_small["router", layer]), "router")
                sc, rk = scores[:, s, :, :], ranked[:, s, :, :]
                lg = banks[:, n, 0:GS * NEXP].rearrange("p (j e) -> p j e", e=NEXP)
                old = past(acc_done, g - 2)
                if layer == 0:
                    bias3 = lambda v: v[:, :].unsqueeze(1).to_broadcast([P, GS, NEXP])
                    t = dve.run(lambda e: e.tensor_tensor(sc, lg, bias3(router_b), ALU.add), t, t_small["bias"], old,
                                signal="route")
                    gen_free[n] = t
                    t = dve.run(lambda e: e.tensor_tensor(rk, sc, bias3(select_b), ALU.add), t, signal="route")
                else:
                    t = dve.run(lambda e: e.tensor_copy(sc, lg), t, old, signal="route")
                    gen_free[n] = t
                    rk = sc
                t_rk = t
                for j in range(GS):
                    t = dve.run(lambda e, j=j: e.max(top_val[:, s, j, :], rk[:, j, :]), t_rk, signal="route")
                t_top = t
                for j in range(GS):
                    t = dve.run(lambda e, j=j: e.max_index(top_idx[:, s, j, :], top_val[:, s, j, :], rk[:, j, :]),
                                t_top, signal="route")
                t = dve.run(lambda e: e.tensor_copy(top_idf[:, s, :, :], top_idx[:, s, :, 0:2]), t, signal="route")
                iota3 = iota8[:, :].unsqueeze(1).to_broadcast([P, GS, NEXP])
                t_idf = t
                for k, hot in ((0, hot1), (1, hot2)):
                    t = dve.run(lambda e, k=k, hot=hot: e.tensor_tensor(
                        hot[:, s, :, :], iota3, top_idf[:, s, :, k:k + 1].to_broadcast([P, GS, NEXP]),
                        ALU.is_equal), t_idf, t_const, signal="route")
                hd, hs = hot_d[:, s, :, :], hot_s[:, s, :, :]
                t = pool.run(lambda e: e.tensor_tensor(hd, hot1[:, s, :, :], hot2[:, s, :, :], ALU.subtract), t,
                             signal="route_pool")
                t = pool.run(lambda e: e.tensor_tensor(hs, hd, sc, ALU.mult), t, signal="route_pool")
                t = dve.run(lambda e: e.tensor_reduce(lead[:, s, :], hs, AX.X, ALU.add), t, signal="route")
                t = act.run(lambda e: e.activation(lead_w[:, s, :], lead[:, s, :], ACT.Tanh, scale=0.5), t,
                            signal="route_act")
                t = pool.run(lambda e: e.tensor_scalar(lead_w[:, s, :], lead_w[:, s, :], 0.5, 0.5, ALU.mult,
                                                       ALU.add), t, signal="route_pool")
                t = pool.run(lambda e: e.tensor_tensor(
                    hs, hd, lead_w[:, s, :].unsqueeze(2).to_broadcast([P, GS, NEXP]), ALU.mult), t,
                    signal="route_pool")
                t = pool.run(lambda e: e.tensor_tensor(hs, hs, hot2[:, s, :, :], ALU.add), t, signal="route_pool")
                t = pool.run(lambda e: e.tensor_scalar(ew[:, s, :, 0:NEXP], hs, gate, None, ALU.mult), t, old,
                             past(ewt_read, g - 2) if layer == 0 else None, signal="route_pool")
                ew_ready[g] = t

            def down_biases(g):
                s = slot_of[g]
                n, free = gen_bank()
                t = pe.run(lambda e: e.transpose(banks[:, n, 0:P], ew[:, s, :, :].rearrange("p j e -> p (j e)"),
                                                 ident[:, :]), ew_ready[g], free, signal="ew_transposed")
                ewt_read[g] = t
                t = act.run(lambda e: e.activation(ew_t[:, s, :], banks[:, n, 0:P], ACT.Copy), t, signal="ew_t")
                gen_free[n] = t
                m, free = gen_bank()
                t = pe.run(lambda e: e.matmul(banks[:, m, :], ew_t[:, s, :], down_bias[:, :, :].rearrange("p j d -> p (j d)"),
                                              start=True, stop=True), t, free, t_small["bias"],
                           signal="down_bias")
                xv = x_res[:, g * GS:(g + 1) * GS, :]
                t = dve.run(lambda e: e.tensor_tensor(
                    xv, banks[:, m, :].rearrange("p (j d) -> p j d", d=D), xv, ALU.add), t,
                    *[x_read[g * GS + j] for j in range(GS)], *[x_ready[g * GS + j] for j in range(GS)],
                    signal="x_down_bias")
                gen_free[m] = t
                for j in range(GS):
                    x_ready[g * GS + j] = t

            def up(g, e8):
                nonlocal up_last_read
                s = slot_of[g]
                h = e8 % 2
                last = g == NG - 1 and False
                tiles = ((0, 2), (1, 3)) if layer == 0 else ((0,), (1,))
                for half, cols in enumerate(tiles):
                    done = {}
                    for c in cols:
                        n = UP_BANK[c] if layer == 0 else UP_BANK[2 * (e8 % 2) + c]
                        done[c] = n, three_pass(
                            banks[:, n, :], up_h[:, e8, c * P:(c + 1) * P], up_l[:, e8, c * P:(c + 1) * P],
                            xt_h[:, s, :], xt_l[:, s, :], (*up_free[n], *xt_ready[s], t_up[layer, e8]), "up")
                        up_last_read = done[c][1]
                    n, t = done[cols[0]]
                    if layer == 0:
                        t = act.run(lambda e, n=n, half=half: e.activation(
                            acted[:, h, half, :], banks[:, n, :], func, bias=up_bias[:, e8, half:half + 1]), t,
                            acted_read.get((h, half)), t_small["bias"], signal="acted")
                        up_free[n] = (t,)
                        nb, tb = done[cols[1]]
                        t = dve.run(lambda e, nb=nb, half=half: e.scalar_tensor_tensor(
                            hidden[:, h, half, :], banks[:, nb, :], up_bias[:, e8, 2 + half:3 + half],
                            acted[:, h, half, :], ALU.add, ALU.mult), tb, t, hidden_read.get(h), signal="hidden")
                        acted_read[h, half] = t
                        up_free[nb] = (t,)
                    else:
                        t = act.run(lambda e, n=n, half=half: e.activation(hidden[:, h, half, :], banks[:, n, :],
                                                                           func), t, hidden_read.get(h),
                                    signal="hidden_act")
                        up_free[n] = (t,)
                    hidden_ready[g, e8, half] = t
                if e8 == NEXP - 1:
                    xt_done[s] = up_last_read

            hidden_ready = {}
            y_turn = [0]

            def down_proj(g, e8):
                s = slot_of[g]
                h = e8 % 2
                n = Y_BANK[y_turn[0] % 2]
                y_turn[0] += 1
                for j in range(GS):
                    for half in (0, 1):
                        t = pe.run(lambda e, j=j, half=half: e.matmul(
                            banks[:, n, j * D:(j + 1) * D], hidden[:, h, half, j * P:(j + 1) * P],
                            down[layer][:, e8, half, :], start=half == 0, stop=half == 1),
                            hidden_ready[g, e8, 0], hidden_ready[g, e8, 1], *y_free[n], t_small["down", layer],
                            signal="y_expert" if (j, half) == (GS - 1, 1) else None)
                hidden_read[h] = t
                for j in range(GS):
                    b = g * GS + j
                    x_ready[b] = dve.run(lambda e, j=j, b=b: e.scalar_tensor_tensor(
                        x_res[:, b, :], banks[:, n, j * D:(j + 1) * D], ew[:, s, j, e8:e8 + 1], x_res[:, b, :],
                        ALU.mult, ALU.add), t, ew_ready[g], x_ready[b], x_read[b], signal="x_moe")
                y_free[n] = (x_ready[g * GS + GS - 1],)
                acc_done[g] = x_ready[g * GS + GS - 1]

            def norm(g):
                slot_of[g] = layernorm_group(g)

            def steps():
                norm(0)
                normalize(0, slot_of[0])
                transpose_norm(slot_of[0])
                route(0)
                yield
                order = [(g, e8) for g in range(NG) for e8 in range(NEXP)]
                for i, (g, e8) in enumerate(order):
                    up(g, e8)
                    if i:
                        down_proj(*order[i - 1])
                        if order[i - 1][1] == NEXP - 1:
                            finish(order[i - 1][0])
                    if e8 == 1 and layer == 0:
                        down_biases(g)
                    if g + 1 < NG:
                        if e8 == 2:
                            norm(g + 1)
                        elif e8 == 3:
                            normalize(g + 1, slot_of[g + 1])
                        elif e8 == 4:
                            transpose_norm(slot_of[g + 1])
                        elif e8 == 5:
                            route(g + 1)
                    yield
                down_proj(*order[-1])
                finish(NG - 1)

            def finish(g):
                if layer == 0:
                    return
                t_out.append(sync.run(lambda e: e.dma_start(
                    out.rearrange("b p d -> p b d")[:, g * GS:(g + 1) * GS, :], x_res[:, g * GS:(g + 1) * GS, :]),
                    *[x_ready[g * GS + j] for j in range(GS)], signal="out", by=16))

            def free_tickets():
                return tuple(t for v in (*up_free.values(), *y_free.values()) for t in v), up_last_read

            return steps(), free_tickets

        t_out = []

        def drive(steps):
            for _ in steps:
                pass

        state = {"q_free": t_ctx_all_transposed, "s_free": None, "pt_free": (None, None), "o_free": None}

        def att(layer):
            drive(attention(layer, state))
            pt = state["pt_free"]
            return (state["s_free"], *pt, state["o_free"])

        load_experts(0, ())
        split_layer1_attention_weights()
        free = att(0)
        m0, m0_free = moe(0, free)
        drive(m0)
        free, up_read = m0_free()
        pe.wait(*free)
        state.update(s_free=None, pt_free=(None, None), o_free=None)
        load_experts(1, (up_read,))
        free = att(1)
        m1, m1_free = moe(1, free)
        drive(m1)
        sync.wait(t_out[-1])

        block = stack.enter_context(nc.Block())

        @block.sync
        def _(eng):
            sync.play(eng)

        @block.tensor
        def _(eng):
            pe.play(eng)

        @block.scalar
        def _(eng):
            act.play(eng)

        @block.vector
        def _(eng):
            dve.play(eng)

        @block.gpsimd
        def _(eng):
            pool.play(eng)


_INS = ["x", "ctx_1024", "g_xattn", "g_ffn",
        "L0_xattn_Wq", "L0_xattn_Wk", "L0_xattn_Wv", "L0_xattn_Wo", "L0_xattn_bo",
        "L0_ffn_Wr", "L0_ffn_br", "L0_ffn_Wl1", "L0_ffn_bl1", "L0_ffn_Wl2", "L0_ffn_bl2", "L0_ffn_biases_N",
        "L1_xattn_Wq", "L1_xattn_bq", "L1_xattn_Wk", "L1_xattn_bk", "L1_xattn_Wv", "L1_xattn_bv",
        "L1_xattn_Wo", "L1_xattn_bo", "L1_ffn_router_w", "L1_ffn_w1", "L1_ffn_w2"]


def kernel(**inputs):
    import numpy as _np
    import concourse.bacc as _bacc
    from concourse import mybir as _mybir
    from concourse.bass_utils import run_bass_kernel_spmd as _run

    nc = _bacc.Bacc("TRN2", target_bir_lowering=False, num_devices=1)
    arrays, args = {}, {}
    for name in _INS:
        arr = _np.ascontiguousarray(inputs[name])
        arrays[f"in_{name}_dram"] = arr
        args[name] = nc.dram_tensor(f"in_{name}_dram", arr.shape, _mybir.dt.from_np(arr.dtype),
                                    kind="ExternalInput").ap()
    shape = arrays["in_x_dram"].shape
    out = nc.dram_tensor("out_0_dram", shape, _mybir.dt.float32, kind="ExternalOutput").ap()
    flamingo_two_layers(nc, args, out)
    r = _run(nc, [arrays], core_ids=[0])
    return r.results[0]["out_0_dram"]
```

```python
from contextlib import ExitStack

import concourse.bass as bass
from concourse import mybir

ALU = mybir.AluOpType
ACT = mybir.ActivationFunctionType
AX = mybir.AxisListType
F32 = mybir.dt.float32
F32R = mybir.dt.float32r
U32 = mybir.dt.uint32

P = 128
EPS = 1e-5
PSUM_BANK = 512
PSUM_BANKS = 8


class Lane:

    def __init__(self, name, counts, semaphore):
        self.name, self.counts, self.semaphore = name, counts, semaphore
        self.steps, self.waited = [], {}

    def wait(self, *tickets):
        for ticket in tickets:
            if ticket is not None and self.waited.get(ticket[0], 0) < ticket[1]:
                self.waited[ticket[0]] = ticket[1]
                self.steps.append(("wait", *ticket, 0))

    def run(self, emit, *tickets, signal=None, by=1):
        self.wait(*tickets)
        self.steps.append(("do", emit, signal, by))
        if signal is None:
            return None
        self.semaphore(signal)
        self.counts[signal] = self.counts.get(signal, 0) + by
        return signal, self.counts[signal]

    def play(self, eng):
        for kind, what, arg, by in self.steps:
            if kind == "wait":
                eng.wait_ge(self.semaphore(what), arg)
            else:
                ins = what(eng)
                if arg is not None:
                    ins.then_inc(self.semaphore(arg), by)


def flamingo_two_layers(nc, a, out):
    x_dram, ctx_dram = a["x"], a["ctx_1024"]
    NSEQ, SEQ, D = x_dram.shape
    _, NKEY, _ = ctx_dram.shape
    INNER0 = a["L0_xattn_Wq"].shape[1]
    NEXP, _, TWOH0 = a["L0_ffn_Wl1"].shape
    HID1 = a["L1_ffn_w1"].shape[2]
    DK0, DK1 = 64, 8
    NH0, NH1 = INNER0 // DK0, D // DK1
    UH = 8
    HALVES1 = NH1 // UH
    GS = 4
    NG = NSEQ // GS
    GT = GS * SEQ
    GK = GS * NKEY
    CTX_ROWS = NSEQ * NKEY
    CTX_BLOCKS = (CTX_ROWS + P - 1) // P
    ROW1 = 4 * DK1
    UNIT_ROWS = UH * NKEY
    CHUNKS = (UNIT_ROWS + P - 1) // P
    chunk_rows = [min(P, UNIT_ROWS - c * P) for c in range(CHUNKS)]
    chunk_key = [c * P % NKEY for c in range(CHUNKS)]
    V1_WINDOW = 108
    REP = max(k + n for k, n in zip(chunk_key, chunk_rows))
    REP_COPIES = (REP + NKEY - 1) // NKEY
    assert SEQ == P and D == P and GT == PSUM_BANK and NH0 == UH and NH1 == 2 * UH
    assert TWOH0 == 4 * P and HID1 == 2 * P and NEXP == 8

    with ExitStack() as stack:
        def sbuf(name, shape, dt=F32):
            return stack.enter_context(nc.sbuf_tensor(name, shape, dt))

        semaphores = {}

        def semaphore(name):
            if name not in semaphores:
                semaphores[name] = stack.enter_context(nc.semaphore(name))
            return semaphores[name]

        counts = {}
        sync = Lane("sync", counts, semaphore)
        pe = Lane("pe", counts, semaphore)
        act = Lane("act", counts, semaphore)
        dve = Lane("dve", counts, semaphore)
        pool = Lane("pool", counts, semaphore)

        def load(lane, dst, src, name, scattered=False):
            return lane.run(lambda e: e.dma_start(dst, src, allow_slow_non_contiguous=scattered),
                            signal="in_" + name, by=16)

        x_res = sbuf("x_res", [P, NSEQ, D])
        ident = sbuf("ident", [P, P])
        iota8 = sbuf("iota8", [P, NEXP])
        head_mask = sbuf("head_mask", [P, 4])
        gates_raw = sbuf("gates_raw", [P, 4])
        gates = sbuf("gates", [P, 4])
        minus_half = sbuf("minus_half", [P, GS])
        ctx_th = sbuf("ctx_th", [P, CTX_ROWS], F32R)
        ctx_tl = sbuf("ctx_tl", [P, CTX_ROWS], F32R)

        wqk_h = sbuf("wqk_h", [P, NH0, D], F32R)
        wqk_l = sbuf("wqk_l", [P, NH0, D], F32R)
        wvo_h = sbuf("wvo_h", [P, NH0, D], F32R)
        wvo_l = sbuf("wvo_l", [P, NH0, D], F32R)
        wq1_h, wq1_l = sbuf("wq1_h", [P, D], F32R), sbuf("wq1_l", [P, D], F32R)
        wk1_h, wk1_l = sbuf("wk1_h", [P, D], F32R), sbuf("wk1_l", [P, D], F32R)
        wv1_h, wv1_l = sbuf("wv1_h", [P, D], F32R), sbuf("wv1_l", [P, D], F32R)
        wo1 = sbuf("wo1", [P, D])
        bq1 = sbuf("bq1", [P, 1])
        bk1 = sbuf("bk1", [P, 1])
        bv1 = sbuf("bv1", [P, 1])
        bo = [sbuf("bo0", [P, D]), sbuf("bo1", [P, D])]

        up_h = sbuf("up_h", [P, NEXP, TWOH0], F32R)
        up_l = sbuf("up_l", [P, NEXP, TWOH0], F32R)
        with nc.sbuf_tensor("ctx_raw", [P, CTX_BLOCKS, D], F32) as ctx_raw:
            ctx_stage = ctx_raw[:, :, :]
        down = [sbuf("down0", [P, NEXP, 2, D]), sbuf("down1", [P, NEXP, 2, D])]
        up_bias = sbuf("up_bias", [P, NEXP, 4])
        down_bias = sbuf("down_bias", [P, GS, D])
        router = [sbuf(f"router{l}", [P, NEXP]) for l in (0, 1)]
        router_h = [sbuf(f"router{l}_h", [P, NEXP], F32R) for l in (0, 1)]
        router_l = [sbuf(f"router{l}_l", [P, NEXP], F32R) for l in (0, 1)]
        router_b = sbuf("router_b", [P, NEXP])
        select_b = sbuf("select_b", [P, NEXP])

        stats = sbuf("stats", [P, 2, GS, 6])
        mean_var = sbuf("mean_var", [P, 2, GS, 2])
        rstd = sbuf("rstd", [P, 2, GS])
        x_norm = sbuf("x_norm", [P, 2, GS, D])
        xt_h = sbuf("xt_h", [P, 2, GT], F32R)
        xt_l = sbuf("xt_l", [P, 2, GT], F32R)

        row_head = sbuf("row_head", [P, CHUNKS, UH])
        prob = sbuf("prob", [P, 2, UH, NKEY])
        prob_t = sbuf("prob_t", [P, 2, UH, SEQ])
        row_max = sbuf("row_max", [P, 2, UH])
        inv_sum = sbuf("inv_sum", [P, 2, NH1])
        row_sum = sbuf("row_sum", [P, 2, UH])
        o_sb = sbuf("o_sb", [P, 2, D])
        o_t = sbuf("o_t", [P, 2, SEQ])

        scores = sbuf("scores", [P, 2, GS, NEXP])
        ranked = sbuf("ranked", [P, 2, GS, NEXP])
        top_val = sbuf("top_val", [P, 2, GS, 8])
        top_idx = sbuf("top_idx", [P, 2, GS, 8], U32)
        top_idf = sbuf("top_idf", [P, 2, GS, 2])
        hot1 = sbuf("hot1", [P, 2, GS, NEXP])
        hot2 = sbuf("hot2", [P, 2, GS, NEXP])
        hot_d = sbuf("hot_d", [P, 2, GS, NEXP])
        hot_s = sbuf("hot_s", [P, 2, GS, NEXP])
        lead = sbuf("lead", [P, 2, GS])
        lead_w = sbuf("lead_w", [P, 2, GS])
        ew = sbuf("ew", [P, 2, GS, 32])
        ew_t = sbuf("ew_t", [P, 2, P])
        acted = sbuf("acted", [P, 2, 2, GT])
        hidden = sbuf("hidden", [P, 2, 2, GT])
        up_raw = sbuf("up_raw", [P, 2, TWOH0])

        layer0_only = ExitStack()
        k0_t = layer0_only.enter_context(nc.sbuf_tensor("k0_t", [P, 2, 2, GS, NH0, NKEY], F32R))
        vo0 = layer0_only.enter_context(nc.sbuf_tensor("vo0", [NKEY, 2, NH0, D], F32))
        layer0_only.close()
        q1_t = sbuf("q1_t", [P, 2, 2, GT], F32R)
        k1_t = sbuf("k1_t", [P, 2, 2, GK], F32R)
        k1_diag = sbuf("k1_diag", [P, 2, 2, GS, 4, NKEY], F32R)
        V1_SIZE = 2 * HALVES1 * CHUNKS * UH * (DK1 + 1)
        v1_flat = sbuf("v1_flat", [P, V1_SIZE])
        v1_rows = v1_flat[:, :].rearrange("p (r t c h d) -> p r t c h d", r=2, t=HALVES1, c=CHUNKS, h=UH)
        v1_t = sbuf("v1_t", [P, GS, REP_COPIES, NKEY])
        v1_raw = sbuf("v1_raw", [P, CHUNKS, HALVES1, UH, DK1])
        prob_extra = sbuf("prob_extra", [P, UH, NKEY])

        banks = stack.enter_context(nc.psum_tensor("banks", [P, PSUM_BANKS, PSUM_BANK], F32))

        def past(tickets, n, *rest, first=None):
            return first if n < 0 else tickets[(n, *rest) if rest else n]

        def split_weight(lane, name, stage, hi, lo, *after):
            th = lane.run(lambda e: e.tensor_copy(hi, stage), *after, signal=name + "_hi")
            return lane.run(lambda e: e.tensor_tensor(lo, stage, hi.bitcast(F32), ALU.subtract), th,
                            signal=name + "_lo")

        raw = [view[:, i, j, :] for view in (acted, hidden) for i in (0, 1) for j in (0, 1)]
        ctx_flat = ctx_dram.rearrange("b k d -> (b k) d")
        full_blocks = CTX_ROWS // P
        t_x = []
        xg = x_dram.rearrange("b p d -> p b d")
        t_x.append(load(sync, x_res[:, 0:GS, :], xg[:, 0:GS, :], "x0"))
        t_ctx = {}
        for first in range(0, full_blocks, 4):
            last = min(first + 4, full_blocks)
            t_ctx[first] = load(act, ctx_stage[:, first:last, :],
                                ctx_flat[first * P:last * P, :].rearrange("(n p) d -> p n d", p=P), f"ctx{first}")
        tail = CTX_ROWS - full_blocks * P
        t_ctx_tail = load(act, ctx_stage[0:tail, full_blocks, :], ctx_flat[full_blocks * P:, :], "ctx_tail")
        raw_w = {}
        t_raw = {}
        for slot, (name, src) in enumerate((("wk0", a["L0_xattn_Wk"]), ("wq0", a["L0_xattn_Wq"]),
                                            ("wv0", a["L0_xattn_Wv"]))):
            raw_w[name] = raw[slot]
            t_raw[name] = load(sync, raw_w[name], src, name)
        raw_w["wo0"] = raw[3].rearrange("p (t n) -> p t n", n=D)
        t_raw["wo0"] = load(sync, raw_w["wo0"], a["L0_xattn_Wo"].rearrange("(t p) n -> p t n", p=P), "wo0")
        t_gates_x = load(act, gates_raw[:, 0:2], a["g_xattn"].partition_broadcast(P), "g_xattn")
        t_gates_f = load(act, gates_raw[:, 2:4], a["g_ffn"].partition_broadcast(P), "g_ffn")
        t_bo = [load(sync, bo[l][:, :], a[f"L{l}_xattn_bo"].partition_broadcast(P), f"bo{l}") for l in (0, 1)]
        t_wo1 = load(sync, wo1[:, :], a["L1_xattn_Wo"], "wo1")
        for g in range(1, NG):
            t_x.append(load(sync, x_res[:, g * GS:(g + 1) * GS, :], xg[:, g * GS:(g + 1) * GS, :], f"x{g}"))
        for place, name in enumerate(("Wq", "Wk", "Wv")):
            key = name.lower() + "1"
            raw_w[key] = raw[4][:, place * D:(place + 1) * D]
            t_raw[key] = load(sync, raw_w[key], a[f"L1_xattn_{name}"], key)

        t_ident0 = pool.run(lambda e: e.memset(ident[:, :], 0.0), signal="ident")
        t_ident = pool.run(lambda e: e.affine_select(
            out=ident[:, :], in_=ident[:, :], compare_op=ALU.not_equal, fill=1.0, base=0,
            pattern=[[-1, P]], channel_multiplier=1), t_ident0, signal="ident")
        t_mhalf = pool.run(lambda e: e.memset(minus_half[:, :], -0.5), signal="constants")
        t_const = t_mhalf
        for e8 in range(NEXP):
            t_const = pool.run(lambda e, e8=e8: e.memset(iota8[:, e8:e8 + 1], float(e8)), signal="constants")
        rh = row_head[:, :, :]
        t_rh = pool.run(lambda e: e.memset(rh, 1.0), signal="row_head")
        t_rh = pool.run(lambda e: e.affine_select(
            out=rh, in_=rh, compare_op=ALU.is_ge, fill=0.0, base=0, pattern=[[P, CHUNKS], [-NKEY, UH]],
            channel_multiplier=1), t_rh, signal="row_head")
        t_row_head = pool.run(lambda e: e.affine_select(
            out=rh, in_=rh, compare_op=ALU.is_ge, fill=0.0, base=NKEY - 1, pattern=[[-P, CHUNKS], [NKEY, UH]],
            channel_multiplier=-1), t_rh, signal="row_head")
        hm = head_mask[:, :]
        t_mask = pool.run(lambda e: e.memset(hm, 1.0), signal="head_mask")
        for i in range(4):
            q = head_mask[ROW1 * i:ROW1 * (i + 1), :]
            t_q = pool.run(lambda e, q=q: e.affine_select(
                out=q, in_=q, compare_op=ALU.is_ge, fill=0.0, base=0, pattern=[[-DK1, 4]], channel_multiplier=1),
                t_mask, signal="head_mask_part")
            t_mask_last = pool.run(lambda e, q=q: e.affine_select(
                out=q, in_=q, compare_op=ALU.is_ge, fill=0.0, base=DK1 - 1, pattern=[[DK1, 4]],
                channel_multiplier=-1), t_q, signal="head_mask_part")
        t_mask = t_mask_last
        t_const = pool.run(lambda e: e.memset(ew[:, :, :, :], 0.0), t_mask, signal="constants")
        load(sync, bq1[:, :], a["L1_xattn_bq"].rearrange("(p o) -> p o", o=1), "bqkv1", scattered=True)
        load(sync, bv1[:, :], a["L1_xattn_bv"].rearrange("(p o) -> p o", o=1), "bqkv1", scattered=True)
        t_bqkv1 = load(sync, bk1[:, :], a["L1_xattn_bk"].rearrange("(p o) -> p o", o=1), "bqkv1", scattered=True)
        t_db_zero = pool.run(lambda e: e.memset(down_bias[:, :, :], 0.0), signal="constants")

        GEN = list(range(PSUM_BANKS))
        bank_free = {n: None for n in range(PSUM_BANKS)}
        gen_turn = [0]

        def gen_bank():
            n = GEN[gen_turn[0] % len(GEN)]
            gen_turn[0] += 1
            return n, bank_free[n]

        t_ctx_t = {}
        t_ctx_read = []

        def transpose_ctx(first):
            n, free = gen_bank()
            last = min(first + 4, CTX_BLOCKS)
            for j in range(first, last):
                rows = min(P, CTX_ROWS - j * P)
                t = pe.run(lambda e, j=j, rows=rows: e.transpose(
                    banks[:, n, (j - first) * P:(j - first) * P + rows], ctx_stage[0:rows, j, :],
                    ident[0:rows, 0:rows]), free, t_ident, t_ctx[first], t_ctx_tail if j == full_blocks else None,
                    signal="ctx_transposed" if j == last - 1 else None)
            t_ctx_read.append(t)
            c0, c1 = first * P, min(last * P, CTX_ROWS)
            th = act.run(lambda e: e.activation(ctx_th[:, c0:c1], banks[:, n, 0:c1 - c0], ACT.Copy), t,
                         signal="ctx_th")
            t_ctx_t[first // 4] = bank_free[n] = dve.run(lambda e: e.tensor_tensor(
                ctx_tl[:, c0:c1], banks[:, n, 0:c1 - c0], ctx_th[:, c0:c1].bitcast(F32), ALU.subtract), th,
                signal="ctx_tl")

        def ctx_ready(row_end):
            return t_ctx_t[(row_end - 1) // (4 * P)]

        t_w = {}
        w_t = {}

        def transpose_weight(slot, name):
            n, free = gen_bank()
            w_t[name] = raw[slot]
            for blk in range(INNER0 // P):
                t = pe.run(lambda e, blk=blk: e.transpose(
                    banks[:, n, blk * P:(blk + 1) * P], raw_w[name][:, blk * P:(blk + 1) * P], ident[:, :]),
                    t_raw[name], t_ident, free, signal="weight_transposed")
            if name == "wk0":
                t = act.run(lambda e: e.activation(w_t[name], banks[:, n, :], ACT.Copy), t,
                            signal="weight_t_" + name)
            else:
                t = dve.run(lambda e: e.tensor_copy(w_t[name], banks[:, n, :]), t,
                            signal="weight_t_" + name)
            bank_free[n] = t
            t_w[name] = t

        def head_products(name, left, right, hi, lo, *after):
            for k in (0, 1):
                n, free = gen_bank()
                rows = slice(DK0 * k, DK0 * (k + 1))
                for blk in range(NH0 // 2):
                    t = pe.run(lambda e, n=n, blk=blk, rows=rows: e.matmul(
                        banks[:, n, blk * D:(blk + 1) * D], left(rows, blk), right(rows, blk),
                        start=True, stop=True, tile_position=(rows.start, 0)), free, *after,
                        signal=name + "_product")
                src = banks[:, n, :].rearrange("p (h d) -> p h d", d=D)
                mine = lambda v, k=k: v[:, k:NH0:2, :]
                t = act.run(lambda e, src=src, mine=mine: e.activation(mine(hi), src, ACT.Copy), t,
                            signal=name + "_hi")
                t_w[name] = bank_free[n] = dve.run(lambda e, src=src, mine=mine: e.tensor_tensor(
                    mine(lo), src, mine(hi).bitcast(F32), ALU.subtract), t, signal=name + "_lo")

        def split_layer1_attention_weights():
            for name, hi, lo in (("wq1", wq1_h, wq1_l), ("wk1", wk1_h, wk1_l), ("wv1", wv1_h, wv1_l)):
                t_w[name] = split_weight(pool, name, raw_w[name], hi[:, :], lo[:, :], t_raw[name])

        up_raw_free = {}
        t_up = {}
        t_small = {}
        up_read = {}

        def load_tables(layer):
            src_down = a["L0_ffn_Wl2"] if layer == 0 else a["L1_ffn_w2"]
            sync.wait(t_ctx_read[-1])
            t_small["down", layer] = load(sync, down[layer][:, :, :, :],
                                          src_down.rearrange("e (t p) d -> p e t d", p=P), f"down{layer}")
            src_router = a["L0_ffn_Wr"] if layer == 0 else a["L1_ffn_router_w"]
            t_small["router_raw", layer] = load(sync, router[layer][:, :], src_router.rearrange("n d -> d n"),
                                                f"router{layer}", scattered=True)
            if layer == 0:
                load(sync, up_bias[:, :, :], a["L0_ffn_bl1"].rearrange("e (t p) -> p e t", p=P), "moe_bias",
                     scattered=True)
                sync.wait(t_db_zero)
                for i in range(GS):
                    load(sync, down_bias[32 * i:32 * i + NEXP, i, :], a["L0_ffn_bl2"], "moe_bias")
                load(sync, router_b[:, :], a["L0_ffn_br"].partition_broadcast(P), "moe_bias")
                t_small["bias"] = load(sync, select_b[:, :], a["L0_ffn_biases_N"].partition_broadcast(P),
                                       "moe_bias")
            fetch_expert(layer, 0)

        def split_router(layer):
            t_small["router", layer] = split_weight(pool, f"router{layer}", router[layer][:, :], router_h[layer][:, :],
                                                    router_l[layer][:, :], t_small["router_raw", layer])

        up_fetched = {}

        def up_stage(layer, e8):
            return up_raw[:, e8 % 2, 0:TWOH0 if layer == 0 else HID1]

        def fetch_expert(layer, e8):
            src = (a["L0_ffn_Wl1"] if layer == 0 else a["L1_ffn_w1"])[e8]
            up_fetched[e8] = sync.run(lambda e: e.dma_start(up_stage(layer, e8), src), up_raw_free.get(e8 % 2),
                                      signal=f"in_up_slot{e8 % 2}", by=16)

        def load_expert(layer, e8):
            if e8 + 1 < NEXP:
                fetch_expert(layer, e8 + 1)
            width = TWOH0 if layer == 0 else HID1
            t_up[layer, e8] = up_raw_free[e8 % 2] = split_weight(
                pool, "up_split", up_stage(layer, e8), up_h[:, e8, 0:width], up_l[:, e8, 0:width],
                up_fetched[e8], up_read.get(e8))

        x_ready = {b: t_x[b // GS] for b in range(NSEQ)}
        x_read = {b: None for b in range(NSEQ)}
        xt_done = {0: None, 1: None}
        xt_ready = {}
        norm_turn = [0]

        def layernorm_group(g):
            s = norm_turn[0] % 2
            norm_turn[0] += 1
            seqs = [g * GS + j for j in range(GS)]
            for j, b in enumerate(seqs):
                t_stats = dve.run(lambda e, b=b, j=j: e.bn_stats(stats[:, s, j, :], x_res[:, b, :]), x_ready[b],
                                  signal="ln_stats")
            for j in range(GS):
                t_mv = dve.run(lambda e, j=j: e.bn_aggr(mean_var[:, s, j, :], stats[:, s, j, :]), t_stats,
                               ln_free[s], signal="ln_mean_var")
            t_eps = pool.run(lambda e: e.tensor_scalar(rstd[:, s, :], mean_var[:, s, :, 1], EPS, None, ALU.add),
                             t_mv, ln_free[s], signal="ln_eps")
            t_rstd = pool.run(lambda e: e.tensor_tensor(rstd[:, s, :], rstd[:, s, :], minus_half[:, :], ALU.pow),
                              t_eps, t_mhalf, signal="ln_rstd")
            norm_ready[s] = t_rstd
            return s

        def normalize(g, s):
            for j in range(GS):
                b = g * GS + j
                t = dve.run(lambda e, b=b, j=j: e.tensor_scalar(
                    x_norm[:, s, j, :], x_res[:, b, :], mean_var[:, s, j, 0:1], rstd[:, s, j:j + 1],
                    ALU.subtract, ALU.mult), norm_ready[s], ln_free[s], x_ready[b], signal="ln_out")
                x_read[b] = t
            norm_ready[s] = t

        def transpose_norm(s):
            t_norm = norm_ready[s]
            n, free = gen_bank()
            for j in range(GS):
                t = pe.run(lambda e, j=j: e.transpose(banks[:, n, j * P:(j + 1) * P], x_norm[:, s, j, :],
                                                      ident[:, :]), t_norm, free, t_ident,
                           signal="ln_transposed" if j == GS - 1 else None)
            ln_free[s] = t
            t_h = act.run(lambda e: e.activation(xt_h[:, s, :], banks[:, n, :], ACT.Copy), t, xt_done[s],
                          signal="xt_h")
            t_l = dve.run(lambda e: e.tensor_tensor(xt_l[:, s, :], banks[:, n, :], xt_h[:, s, :].bitcast(F32),
                                                    ALU.subtract), t_h, xt_done[s], signal="xt_l")
            bank_free[n] = t_l
            xt_ready[s] = (t_h, t_l)

        norm_ready = {}
        ln_free = {0: None, 1: None}

        def three_pass(outp, wh, wl, xh, xl, tickets, signal):
            pe.run(lambda e: e.matmul(outp, wh, xh, start=True, stop=False), *tickets)
            pe.run(lambda e: e.matmul(outp, wl, xh, start=False, stop=False))
            return pe.run(lambda e: e.matmul(outp, wh, xl, start=False, stop=True), signal=signal)

        S_BANK = (0, 1)
        PT_BANK = (2, 3)
        O_BANK = 4
        ATTENTION_GEN = (6, 7, 5)

        qk_free = {0: None}

        def attention(layer):
            DK = (DK0, DK1)[layer]
            NH = (NH0, NH1)[layer]
            DV1 = DK + 1
            HALVES = NH // UH
            SCALE = float(DK) ** -0.5

            PROB_RING = (2, 3)[layer]
            PROB_LAG = (1, 2)[layer]

            def prob_of(u):
                return prob_extra[:, :, :] if u % PROB_RING == 2 else prob[:, u % PROB_RING, :, :]

            units = [(b, h) for b in range(NSEQ) for h in range(HALVES)]
            q_ready, k_ready, v_ready = {}, {}, {}
            scores_done = {}
            pv_done = {}
            sub_done, exp_done, pt_done, pt_copied, norm_done, ot_ready, y_done = {}, {}, {}, {}, {}, {}, {}
            ot_read = {}
            v_read, v_t_ready = {}, {}
            t_v1_ones = None
            last_unit = lambda b: b * HALVES + HALVES - 1
            slot_of = {}

            def q_task(g):
                s = slot_of[g]
                n, free = gen_bank()
                old = past(scores_done, last_unit(g * GS - GS - 1) if g >= 2 else -1, first=qk_free[layer])
                t = three_pass(banks[:, n, :], wq1_h[:, :], wq1_l[:, :], xt_h[:, s, :], xt_l[:, s, :],
                               (free, *xt_ready[s], t_w["wq1"]), "q_proj")
                xt_done[s] = t
                t = act.run(lambda e: e.activation(q1_t[:, g % 2, 0, :], banks[:, n, :], ACT.Identity,
                                                   bias=bq1[:, 0:1]), t, old, t_bqkv1, signal="q_t")
                t = dve.run(lambda e: e.scalar_tensor_tensor(
                    q1_t[:, g % 2, 1, :], banks[:, n, :], bq1[:, 0:1], q1_t[:, g % 2, 0, :].bitcast(F32),
                    ALU.add, ALU.subtract), t, old, t_bqkv1, signal="q_tl")
                bank_free[n] = t
                q_ready[g] = t

            def k0_task(g, head):
                c0 = g * GK
                n, free = gen_bank()
                old = past(scores_done, last_unit(g * GS - GS - 1) if g >= 2 else -1,
                           first=qk_free[layer])
                t = three_pass(banks[:, n, 0:GK], wqk_h[:, head, :], wqk_l[:, head, :],
                               ctx_th[:, c0:c0 + GK], ctx_tl[:, c0:c0 + GK],
                               (free, ctx_ready(c0 + GK), t_w["wqk"]), "k_proj")
                hi, lo = k0_t[:, g % 2, 0, :, head, :], k0_t[:, g % 2, 1, :, head, :]
                k_view = banks[:, n, 0:GK].rearrange("p (j n) -> p j n", n=NKEY)
                t = act.run(lambda e: e.activation(hi, k_view, ACT.Copy), t, old, signal="k_t")
                t = dve.run(lambda e: e.tensor_tensor(lo, k_view, hi.bitcast(F32), ALU.subtract), t, old,
                            signal="k_tl")
                bank_free[n] = t
                k_ready[g] = t

            def k1_task(g):
                c0 = g * GK
                n, free = gen_bank()
                t = three_pass(banks[:, n, 0:GK], wk1_h[:, :], wk1_l[:, :],
                               ctx_th[:, c0:c0 + GK], ctx_tl[:, c0:c0 + GK],
                               (free, ctx_ready(c0 + GK), t_w["wk1"]), "k_proj")
                old = past(k_ready, g - 2, first=qk_free[layer])
                t = act.run(lambda e: e.activation(k1_t[:, g % 2, 0, :], banks[:, n, 0:GK], ACT.Identity,
                                                   bias=bk1[:, 0:1]), t, old, t_bqkv1, signal="k_t")
                t = dve.run(lambda e: e.scalar_tensor_tensor(
                    k1_t[:, g % 2, 1, :], banks[:, n, 0:GK], bk1[:, 0:1], k1_t[:, g % 2, 0, :].bitcast(F32),
                    ALU.add, ALU.subtract), t, old, t_bqkv1, signal="k_tl")
                k_ready[g, "plain"] = bank_free[n] = t

            def k1_diag_task(g, j):
                k_ready[g] = pool.run(lambda e: e.tensor_tensor(
                    k1_diag[:, g % 2, :, j, :, :],
                    k1_t[:, g % 2, :, j * NKEY:(j + 1) * NKEY].bitcast(F32).unsqueeze(2).to_broadcast(
                        [P, 2, 4, NKEY]),
                    head_mask[:, :].unsqueeze(1).unsqueeze(3).to_broadcast([P, 2, 4, NKEY]), ALU.mult),
                    k_ready[g, "plain"], t_mask, past(scores_done, last_unit(g * GS - GS - 1) if g >= 2 else -1,
                                                      first=qk_free[layer]), signal="k1_diag")

            def v1_task(g):
                c0 = g * GK
                n, free = gen_bank()
                t = three_pass(banks[:, n, 0:GK], wv1_h[:, :], wv1_l[:, :],
                               ctx_th[:, c0:c0 + GK], ctx_tl[:, c0:c0 + GK],
                               (free, ctx_ready(c0 + GK), t_w["wv1"]), "v_t")
                v_t_ready[g] = bank_free[n] = act.run(lambda e: e.activation(
                    v1_t[:, :, :, :], banks[:, n, 0:GK].rearrange("p (j n) -> p j n", n=NKEY).unsqueeze(2)
                    .to_broadcast([P, GS, REP_COPIES, NKEY]), ACT.Identity, bias=bv1[:, 0:1]), t, t_bqkv1,
                    past(v_read, g * GS - 1 if g else -1, first=qk_free[1]), signal="v1_t")

            def v_proj(b):
                c0 = b * NKEY
                old = past(pv_done, last_unit(b - 2) if b >= 2 else -1)
                if layer == 0:
                    for h0 in (0, 4):
                        n, free = gen_bank()
                        four = lambda v, h0=h0: v[:, h0:h0 + 4, :].rearrange("p h d -> p (h d)")
                        t = three_pass(banks[0:NKEY, n, :], ctx_th[:, c0:c0 + NKEY], ctx_tl[:, c0:c0 + NKEY],
                                       four(wvo_h), four(wvo_l), (free, ctx_ready(c0 + NKEY), t_w["wvo"]),
                                       "v_proj")
                        t = act.run(lambda e, n=n, four=four: e.activation(
                            four(vo0[:, b % 2, :, :]), banks[0:NKEY, n, :], ACT.Copy), t, old, signal="v")
                        bank_free[n] = t
                else:
                    rep = v1_t[:, b % GS, :, :].rearrange("p r n -> p (r n)")
                    for chunks in (range(0, 4), range(4, CHUNKS)):
                        n, free = gen_bank()
                        for c in chunks:
                            t = pe.run(lambda e, c=c, n=n: e.transpose(
                                banks[0:chunk_rows[c], n, c % 4 * D:(c % 4 + 1) * D],
                                rep[:, chunk_key[c]:chunk_key[c] + chunk_rows[c]], ident[:, :]),
                                free, v_t_ready[b // GS], signal="v_rows" if c == chunks[-1] else None)
                        v_read[b] = t
                        rows, k = chunk_rows[chunks[0]], len(chunks)
                        raw_v = v1_raw[0:rows, chunks[0]:chunks[-1] + 1, :, :, :]
                        flat = raw_v.rearrange("p c t h d -> p (c t h d)")
                        bank_free[n] = t = act.run(lambda e, n=n, flat=flat, rows=rows, k=k: e.activation(
                            flat, banks[0:rows, n, 0:k * D], ACT.Copy), t,
                            v_ready[b - 1] if b else qk_free[1], signal="v1_raw")
                        for half in range(HALVES):
                            dst = v1_rows[0:rows, b % 2, half, chunks[0]:chunks[-1] + 1, :, 0:DK]
                            mask = row_head[0:rows, chunks[0]:chunks[-1] + 1, :].unsqueeze(3).to_broadcast(
                                [rows, k, UH, DK])
                            t = pool.run(lambda e, dst=dst, raw_v=raw_v, mask=mask, half=half: e.tensor_tensor(
                                dst, raw_v[:, :, half, :, :], mask, ALU.mult), t if half == 0 else None, old,
                                t_v1_ones, signal="v1")
                v_ready[b] = t

            def score(u):
                b, half = units[u]
                g, j = b // GS, b % GS
                tok = slice(j * SEQ, (j + 1) * SEQ)
                free = [bank_free[n] for n in S_BANK]
                if layer == 0:
                    s = slot_of[g]
                    passes = [(xt_h, 0, 0), (xt_h, 0, 1), (xt_h, 1, 0), (xt_h, 1, 1), (xt_l, 0, 0), (xt_l, 0, 1)]
                    for i, (q, k_part, k) in enumerate(passes):
                        t = pe.run(lambda e, q=q, k_part=k_part, k=k, i=i: e.matmul(
                            banks[:, S_BANK[k], 0:4 * NKEY], q[:, s, tok],
                            k0_t[:, g % 2, k_part, j, 4 * k:4 * k + 4, :].rearrange("p h n -> p (h n)"),
                            start=i < 2, stop=i >= 4),
                            *xt_ready[s], k_ready[g], *free, signal="scores" if i == 5 else None)
                    xt_done[s] = t
                else:
                    passes = [(0, 0, 0), (0, 0, 1), (0, 1, 0), (0, 1, 1), (1, 0, 0), (1, 0, 1)]
                    for i, (q_part, k_part, k) in enumerate(passes):
                        row = ROW1 * (2 * half + k)
                        t = pe.run(lambda e, q_part=q_part, k_part=k_part, k=k, row=row: e.matmul(
                            banks[:, S_BANK[k], 0:4 * NKEY], q1_t[row:row + ROW1, g % 2, q_part, tok],
                            k1_diag[row:row + ROW1, g % 2, k_part, j, :, :].rearrange("p h n -> p (h n)"),
                            start=(q_part, k_part) == (0, 0), stop=q_part == 1, tile_position=(row, 0)),
                            q_ready[g], k_ready[g], *free, signal="scores" if i == 5 else None)
                scores_done[u] = t
                s_view = banks[:, S_BANK[0]:S_BANK[1] + 1, 0:4 * NKEY].rearrange("p k (s n) -> p k s n", n=NKEY)
                m_view = row_max[:, u % 2, :].rearrange("p (k s) -> p k s", k=2)
                p_view = prob_of(u).rearrange("p (k s) n -> p k s n", k=2)
                t = dve.run(lambda e: e.tensor_reduce(m_view, s_view, AX.X, ALU.max), t, signal="row_max")
                t = dve.run(lambda e: e.tensor_tensor(
                    p_view, s_view, m_view.unsqueeze(3).to_broadcast([P, 2, 4, NKEY]), ALU.subtract), t,
                    past(pt_done, u - PROB_RING), qk_free[1] if layer == 1 and u == 2 else None, signal="shifted")
                for n in S_BANK:
                    bank_free[n] = t
                sub_done[u] = t

            def exponentiate(u):
                exp_done[u] = act.run(lambda e: e.activation(prob_of(u), prob_of(u), ACT.Exp, scale=SCALE),
                                      sub_done[u], signal="exp")

            def divide(u):
                pv, sums, inv = prob[:, u % 2, :, :], row_sum[:, u % 2, :], inv_sum[:, u % 2, 0:UH]
                t = dve.run(lambda e: e.tensor_reduce(sums, pv, AX.X, ALU.add), exp_done[u], signal="row_sum")
                t = dve.run(lambda e: e.reciprocal(inv, sums), t, past(exp_done, u - 2), signal="inv_sum")
                exp_done[u] = pool.run(lambda e: e.tensor_tensor(
                    pv, pv, inv.unsqueeze(2).to_broadcast([P, UH, NKEY]), ALU.mult), t, signal="divided")

            def transpose_prob1(u):
                flat = prob_of(u).rearrange("p h n -> p (h n)")
                for k, chunks in enumerate((range(0, 4), range(4, CHUNKS))):
                    rows = chunk_rows[chunks[0]]
                    for c in chunks:
                        t = pe.run(lambda e, c=c, k=k: e.transpose(
                            banks[0:chunk_rows[c], PT_BANK[k], c % 4 * SEQ:(c % 4 + 1) * SEQ],
                            flat[:, c * P:c * P + chunk_rows[c]], ident[:, :]),
                            exp_done[u], bank_free[PT_BANK[k]],
                            signal="prob_transposed" if c == chunks[-1] else None)
                    dst = prob_t[0:rows, u % 2, chunks[0]:chunks[-1] + 1, :].rearrange("p s n -> p (s n)")
                    src = banks[0:rows, PT_BANK[k], 0:len(chunks) * SEQ]
                    pt_copied[u, k] = bank_free[PT_BANK[k]] = act.run(lambda e, dst=dst, src=src: e.activation(
                        dst, src, ACT.Copy), t, past(pv_done, u - 2), signal="prob_t_act")
                pt_done[u] = t

            def transpose_prob0(u):
                for k in (0, 1):
                    for place in range(4):
                        t = pe.run(lambda e, k=k, place=place: e.transpose(
                            banks[0:NKEY, PT_BANK[k], place * SEQ:(place + 1) * SEQ],
                            prob[:, u % 2, 4 * k + place, :], ident[:, :]),
                            exp_done[u], bank_free[PT_BANK[k]],
                            signal="prob_transposed" if place == 3 else None)
                    dst = prob_t[0:NKEY, u % 2, 4 * k:4 * k + 4, :].rearrange("p s n -> p (s n)")
                    if k == 0 or u % 4 > 0:
                        pt_copied[u, k] = act.run(lambda e, dst=dst, k=k: e.activation(
                            dst, banks[0:NKEY, PT_BANK[k], :], ACT.Copy), t, past(pv_done, u - 2), signal="prob_t_act")
                    else:
                        pt_copied[u, k] = dve.run(lambda e, dst=dst, k=k: e.tensor_copy(
                            dst, banks[0:NKEY, PT_BANK[k], :]), t, past(pv_done, u - 2), signal="prob_t_dve")
                    bank_free[PT_BANK[k]] = pt_copied[u, k]
                pt_done[u] = t

            def weigh_values0(b):
                n = O_BANK
                for head in range(NH0):
                    t = pe.run(lambda e, head=head: e.matmul(
                        banks[:, n, 0:D], prob_t[0:NKEY, b % 2, head, :], vo0[:, b % 2, head, :],
                        start=head == 0, stop=head == NH0 - 1),
                        pt_copied[b, 0], pt_copied[b, 1], v_ready[b], bank_free[n],
                        signal="pv" if head == NH0 - 1 else None)
                pv_done[b] = t
                x_ready[b] = bank_free[n] = dve.run(lambda e: e.scalar_tensor_tensor(
                    x_res[:, b, :], banks[:, n, 0:D], gates[:, 0:1], x_res[:, b, :], ALU.mult, ALU.add), t,
                    x_ready[b], t_gates, signal="x_attn")

            def add_bias(b):
                x_ready[b] = pool.run(lambda e: e.tensor_tensor(x_res[:, b, :], x_res[:, b, :], bo[layer][:, :],
                                                                ALU.add), x_read[b], t_bo_gated[layer], signal="x_bias")

            def weigh_values1(u):
                b, half = units[u]
                s = b % 2
                width = UH * DV1
                for c in range(CHUNKS):
                    rows = chunk_rows[c]
                    first = ((s * HALVES + half) * CHUNKS + c) * width
                    cols = width if (half, c) == (HALVES - 1, CHUNKS - 1) else V1_WINDOW
                    t = pe.run(lambda e, c=c, rows=rows, first=first, cols=cols: e.matmul(
                        banks[:, O_BANK, half * width:half * width + cols], prob_t[0:rows, u % 2, c, :],
                        v1_flat[0:rows, first:first + cols], start=c == 0, stop=c == CHUNKS - 1),
                        pt_copied[u, 0], pt_copied[u, 1], v_ready[b], t_v1_ones, bank_free[O_BANK],
                        signal="pv" if c == CHUNKS - 1 else None)
                pv_done[u] = t
                if half < HALVES - 1:
                    return
                o_view = banks[:, O_BANK, 0:NH * DV1].rearrange("p (h d) -> p h d", d=DV1)
                inv = inv_sum[:, s, :]
                dst = o_sb[:, s, :].rearrange("p (h d) -> p h d", d=DK)
                t = dve.run(lambda e: e.reciprocal(inv, o_view[:, :, DK]), t, signal="inv_sum")
                norm_done[b] = bank_free[O_BANK] = dve.run(lambda e: e.tensor_tensor(
                    dst, o_view[:, :, 0:DK], inv.unsqueeze(2).to_broadcast([P, NH, DK]), ALU.mult), t,
                    past(ot_read, b - 2), signal="o_norm")

            def transpose_o(b):
                n, free = gen_bank()
                ot_read[b] = t = pe.run(lambda e: e.transpose(banks[:, n, 0:P], o_sb[:, b % 2, :], ident[:, :]),
                                        norm_done[b], free, signal="o_transposed")
                ot_ready[b] = bank_free[n] = act.run(lambda e: e.activation(
                    o_t[:, b % 2, :], banks[:, n, 0:P], ACT.Copy), t, past(y_done, b - 2), signal="o_t")

            def project_o(b):
                n, free = gen_bank()
                y_done[b] = t = pe.run(lambda e: e.matmul(banks[:, n, 0:D], o_t[:, b % 2, :], wo1[:, :], start=True,
                                                          stop=True), ot_ready[b], free, t_wo1, signal="y")
                x_ready[b] = bank_free[n] = dve.run(lambda e: e.scalar_tensor_tensor(
                    x_res[:, b, :], banks[:, n, 0:D], gates[:, 1:2], x_res[:, b, :],
                    ALU.mult, ALU.add), t, x_ready[b], t_gates, signal="x_attn")

            def prepare(g):
                if layer == 1 and g == 0:
                    yield set_v1_ones
                yield lambda: slot_of.__setitem__(g, layernorm_group(g))
                if layer == 0:
                    for head in range(NH0):
                        yield lambda head=head: k0_task(g, head)
                        if head == 2:
                            yield lambda: normalize(g, slot_of[g])
                        if head == 5:
                            yield lambda: transpose_norm(slot_of[g])
                else:
                    yield lambda: k1_task(g)
                    yield lambda: normalize(g, slot_of[g])
                    for j in range(GS):
                        yield lambda j=j: k1_diag_task(g, j)
                        if j == 0:
                            yield lambda: transpose_norm(slot_of[g])
                        if j == 1:
                            yield lambda: q_task(g)

            def set_v1_ones():
                nonlocal t_v1_ones
                t = pool.run(lambda e: e.memset(v1_flat[:, :], 0.0), qk_free[1], signal="v1_zero")
                for ring in (0, 1):
                    for half in range(HALVES):
                        ones = v1_rows[:, ring, half, :, :, DK1]
                        t_v1_ones = pool.run(lambda e, ones=ones: e.tensor_copy(ones, row_head[:, :, :]), t_row_head,
                                             t, signal="v1_ones")

            def steps(background, tail):
                per = GS * HALVES
                U = len(units)
                GEN[:], gen_turn[0] = ATTENTION_GEN, 0
                for u in range(U + PROB_LAG + 3):
                    if u < U:
                        b, half = units[u]
                        ahead = u if u == 0 else u + 1
                        if u == 0 or ahead % per == 0:
                            g = ahead // per + 1
                            pending = list(prepare(g)) if g < NG else list(tail) if g == NG else []
                        score(u)
                        if layer == 0:
                            exponentiate(u)
                        left = per - 1 if u == 0 else per - ahead % per
                    if 0 <= u - PROB_LAG - 1 < U:
                        (weigh_values0 if layer == 0 else weigh_values1)(u - PROB_LAG - 1)
                    if layer == 1 and u < U and u % per == 0:
                        v1_task(b // GS)
                    if u < U and half == HALVES - 1:
                        v_proj(b)
                    if 0 <= u - PROB_LAG < U:
                        (transpose_prob0 if layer == 0 else transpose_prob1)(u - PROB_LAG)
                    if u < U and layer == 0:
                        divide(u)
                    if u < U:
                        for _ in range(-(-len(pending) // left)):
                            pending.pop(0)()
                    if u < U and half == 0:
                        add_bias(b)
                    if background:
                        background.pop(0)()
                    if layer == 1:
                        if 0 <= u - 4 < U and units[u - 4][1] == HALVES - 1:
                            transpose_o(units[u - 4][0])
                        if 0 <= u - 5 < U and units[u - 5][1] == HALVES - 1:
                            project_o(units[u - 5][0])
                        if u < U:
                            exponentiate(u)
                    if layer == 0 and u == U + 1:
                        qk_free[1] = pv_done[U - 1]
                    yield

            return prepare, steps

        UP_BANK = (0, 1, 2, 3)
        Y_BANK = (4, 5)
        MOE_GEN = (6, 7)

        def moe(layer):
            func = (ACT.Silu, ACT.Gelu)[layer]
            gate = gates[:, 2 + layer:3 + layer]
            hidden_read = {}
            acted_read = {}
            ew_ready, ewt_read, ewt_ready = {}, {}, {}
            slot_of = {}
            acc_done = {}

            def route(g):
                s = slot_of[g]
                n, free = gen_bank()
                for j in range(GS):
                    th, tl = xt_h[:, s, j * P:(j + 1) * P], xt_l[:, s, j * P:(j + 1) * P]
                    t = three_pass(banks[:, n, j * NEXP:(j + 1) * NEXP], th, tl, router_h[layer][:, :],
                                   router_l[layer][:, :], (free, *xt_ready[s], t_small["router", layer]), "router")
                sc, rk = scores[:, s, :, :], ranked[:, s, :, :]
                lg = banks[:, n, 0:GS * NEXP].rearrange("p (j e) -> p j e", e=NEXP)
                old = past(acc_done, g - 2)
                if layer == 0:
                    bias3 = lambda v: v[:, :].unsqueeze(1).to_broadcast([P, GS, NEXP])
                    t = dve.run(lambda e: e.tensor_tensor(sc, lg, bias3(router_b), ALU.add), t, t_small["bias"], old,
                                signal="route")
                    bank_free[n] = t
                    t = dve.run(lambda e: e.tensor_tensor(rk, sc, bias3(select_b), ALU.add), t, signal="route")
                else:
                    t = dve.run(lambda e: e.tensor_copy(sc, lg), t, old, signal="route")
                    bank_free[n] = t
                    rk = sc
                t_rk = t
                for j in range(GS):
                    t = dve.run(lambda e, j=j: e.max(top_val[:, s, j, :], rk[:, j, :]), t_rk, signal="route")
                t_top = t
                for j in range(GS):
                    t = dve.run(lambda e, j=j: e.max_index(top_idx[:, s, j, :], top_val[:, s, j, :], rk[:, j, :]),
                                t_top, signal="route")
                t = dve.run(lambda e: e.tensor_copy(top_idf[:, s, :, :], top_idx[:, s, :, 0:2]), t, signal="route")
                iota3 = iota8[:, :].unsqueeze(1).to_broadcast([P, GS, NEXP])
                t_idf = t
                for k, hot in ((0, hot1), (1, hot2)):
                    t = dve.run(lambda e, k=k, hot=hot: e.tensor_tensor(
                        hot[:, s, :, :], iota3, top_idf[:, s, :, k:k + 1].to_broadcast([P, GS, NEXP]),
                        ALU.is_equal), t_idf, t_const, signal="route")
                hd, hs = hot_d[:, s, :, :], hot_s[:, s, :, :]
                t = pool.run(lambda e: e.tensor_tensor(hd, hot1[:, s, :, :], hot2[:, s, :, :], ALU.subtract), t,
                             signal="route_pool")
                t = pool.run(lambda e: e.tensor_tensor(hs, hd, sc, ALU.mult), t, signal="route_pool")
                t = dve.run(lambda e: e.tensor_reduce(lead[:, s, :], hs, AX.X, ALU.add), t, signal="route")
                t = act.run(lambda e: e.activation(lead_w[:, s, :], lead[:, s, :], ACT.Tanh, scale=0.5), t,
                            signal="route_act")
                t = pool.run(lambda e: e.tensor_scalar(lead_w[:, s, :], lead_w[:, s, :], 0.5, 0.5, ALU.mult,
                                                       ALU.add), t, signal="route_pool")
                t = pool.run(lambda e: e.tensor_tensor(
                    hs, hd, lead_w[:, s, :].unsqueeze(2).to_broadcast([P, GS, NEXP]), ALU.mult), t,
                    signal="route_pool")
                t = pool.run(lambda e: e.tensor_tensor(hs, hs, hot2[:, s, :, :], ALU.add), t, signal="route_pool")
                t = pool.run(lambda e: e.tensor_scalar(ew[:, s, :, 0:NEXP], hs, gate, None, ALU.mult), t, old,
                             past(ewt_read, g - 2) if layer == 0 else None, signal="route_pool")
                ew_ready[g] = t

            def transpose_ew(g):
                s = slot_of[g]
                n, free = gen_bank()
                t = pe.run(lambda e: e.transpose(banks[:, n, 0:P], ew[:, s, :, :].rearrange("p j e -> p (j e)"),
                                                 ident[:, :]), ew_ready[g], free, signal="ew_transposed")
                ewt_read[g] = t
                t = act.run(lambda e: e.activation(ew_t[:, s, :], banks[:, n, 0:P], ACT.Copy), t, signal="ew_t")
                bank_free[n] = ewt_ready[g] = t

            def down_biases(g):
                s = slot_of[g]
                m, free = gen_bank()
                t = pe.run(lambda e: e.matmul(banks[:, m, :], ew_t[:, s, :], down_bias[:, :, :].rearrange("p j d -> p (j d)"),
                                              start=True, stop=True), ewt_ready[g], free, t_small["bias"],
                           signal="down_bias")
                xv = x_res[:, g * GS:(g + 1) * GS, :]
                t = dve.run(lambda e: e.tensor_tensor(
                    xv, banks[:, m, :].rearrange("p (j d) -> p j d", d=D), xv, ALU.add), t,
                    *[x_read[g * GS + j] for j in range(GS)], *[x_ready[g * GS + j] for j in range(GS)],
                    signal="x_down_bias")
                bank_free[m] = t
                for j in range(GS):
                    x_ready[g * GS + j] = t

            def up(g, e8):
                s = slot_of[g]
                h = e8 % 2
                tiles = ((0, 2), (1, 3)) if layer == 0 else ((0,), (1,))
                for half, cols in enumerate(tiles):
                    done = {}
                    for k, c in enumerate(cols):
                        n = UP_BANK[2 * half + k] if layer == 0 else UP_BANK[2 * (e8 % 2) + c]
                        done[c] = n, three_pass(
                            banks[:, n, :], up_h[:, e8, c * P:(c + 1) * P], up_l[:, e8, c * P:(c + 1) * P],
                            xt_h[:, s, :], xt_l[:, s, :], (bank_free[n], *xt_ready[s], t_up[layer, e8]), "up")
                        xt_done[s] = up_read[e8] = done[c][1]
                    n, t = done[cols[0]]
                    if layer == 0:
                        t = act.run(lambda e, n=n, half=half: e.activation(
                            acted[:, h, half, :], banks[:, n, :], func, bias=up_bias[:, e8, half:half + 1]), t,
                            acted_read.get((h, half)), t_small["bias"], signal="acted")
                        bank_free[n] = t
                        nb, tb = done[cols[1]]
                        t = dve.run(lambda e, nb=nb, half=half: e.scalar_tensor_tensor(
                            hidden[:, h, half, :], banks[:, nb, :], up_bias[:, e8, 2 + half:3 + half],
                            acted[:, h, half, :], ALU.add, ALU.mult), tb, t, hidden_read.get(h), signal="hidden")
                        acted_read[h, half] = t
                        bank_free[nb] = t
                    else:
                        t = act.run(lambda e, n=n, half=half: e.activation(hidden[:, h, half, :], banks[:, n, :],
                                                                           func), t, hidden_read.get(h),
                                    signal="hidden_act")
                        bank_free[n] = t
                    hidden_ready[g, e8, half] = t
                    yield

            hidden_ready = {}
            y_turn = [0]

            def down_proj(g, e8):
                s = slot_of[g]
                h = e8 % 2
                n = Y_BANK[y_turn[0] % 2]
                y_turn[0] += 1
                for j in range(GS):
                    for half in (0, 1):
                        t = pe.run(lambda e, j=j, half=half: e.matmul(
                            banks[:, n, j * D:(j + 1) * D], hidden[:, h, half, j * P:(j + 1) * P],
                            down[layer][:, e8, half, :], start=half == 0, stop=half == 1),
                            hidden_ready[g, e8, 0], hidden_ready[g, e8, 1], bank_free[n], t_small["down", layer],
                            signal="y_expert" if (j, half) == (GS - 1, 1) else None)
                hidden_read[h] = t
                for j in range(GS):
                    b = g * GS + j
                    x_ready[b] = dve.run(lambda e, j=j, b=b: e.scalar_tensor_tensor(
                        x_res[:, b, :], banks[:, n, j * D:(j + 1) * D], ew[:, s, j, e8:e8 + 1], x_res[:, b, :],
                        ALU.mult, ALU.add), t, ew_ready[g], x_ready[b], x_read[b], signal="x_moe")
                bank_free[n] = acc_done[g] = x_ready[g * GS + GS - 1]

            def norm(g):
                slot_of[g] = layernorm_group(g)

            def prepare(g):
                return [lambda: norm(g), lambda: normalize(g, slot_of[g]), lambda: transpose_norm(slot_of[g]),
                        lambda: route(g)]

            no_task = lambda: None

            def steps(tail, expert_done):
                GEN[:] = MOE_GEN
                order = [(g, e8) for g in range(NG) for e8 in range(NEXP)]
                for i, (g, e8) in enumerate(order):
                    yield from up(g, e8)
                    if g == NG - 1:
                        expert_done(e8)
                    if i:
                        down_proj(*order[i - 1])
                        if order[i - 1][1] == NEXP - 1:
                            finish(order[i - 1][0])
                    if e8 == 1 and layer == 0:
                        transpose_ew(g)
                    if e8 == 2 and layer == 0:
                        down_biases(g)
                    if e8 == 1:
                        pending = prepare(g + 1) + [no_task] * 2 if g + 1 < NG else list(tail)
                    if e8 >= 2:
                        for _ in range(-(-len(pending) // (NEXP - e8))):
                            pending.pop(0)()
                    yield
                down_proj(*order[-1])
                finish(NG - 1)

            def finish(g):
                if layer == 0:
                    return
                t_out.append(sync.run(lambda e: e.dma_start(
                    out.rearrange("b p d -> p b d")[:, g * GS:(g + 1) * GS, :], x_res[:, g * GS:(g + 1) * GS, :]),
                    *[x_ready[g * GS + j] for j in range(GS)], signal="out", by=16))

            return prepare, steps

        t_out = []

        att_prepare, att_steps = zip(*[attention(layer) for layer in (0, 1)])
        moe_prepare, moe_steps = zip(*[moe(layer) for layer in (0, 1)])

        block_of = lambda v: (lambda rows, blk: v[rows, blk * P:(blk + 1) * P])
        first_tasks = list(att_prepare[0](0))
        first_tasks.pop(0)()
        transpose_weight(5, "wk0")
        transpose_weight(6, "wq0")
        transpose_ctx(0)
        head_products("wqk", block_of(w_t["wk0"]), block_of(w_t["wq0"]), wqk_h, wqk_l, t_w["wq0"], t_w["wk0"])
        transpose_weight(7, "wv0")
        for task in first_tasks:
            task()
        head_products("wvo", block_of(w_t["wv0"]), lambda rows, blk: raw_w["wo0"][rows, blk, :], wvo_h, wvo_l,
                      t_w["wv0"], t_raw["wo0"])
        transpose_ctx(4)
        t_gates = act.run(lambda e: e.activation(gates[:, :], gates_raw[:, :], ACT.Tanh), t_gates_x, t_gates_f,
                       signal="gates")
        t_bo_gated = [pool.run(lambda e, l=l: e.tensor_scalar(
            bo[l][:, :], bo[l][:, :], gates[:, l:l + 1], None, ALU.mult), t_gates, t_bo[l], signal="bo_gated")
            for l in (0, 1)]

        background = [*[lambda first=first: transpose_ctx(first) for first in range(8, CTX_BLOCKS, 4)],
                      lambda: load_tables(0), *[lambda e8=e8: load_expert(0, e8) for e8 in range(NEXP)],
                      split_layer1_attention_weights, lambda: split_router(0), lambda: load_tables(1),
                      lambda: split_router(1)]
        units = [NSEQ * heads // UH for heads in (NH0, NH1)]
        moe_alone = NG * NEXP * 3
        attend = [att_steps[0](background, moe_prepare[0](0)), att_steps[1]([], moe_prepare[1](0))]
        mix = [moe_steps[0](list(att_prepare[1](0)), lambda e8: load_expert(1, e8)),
               moe_steps[1]([], lambda e8: None)]
        done = 0
        for phase, nxt, alone in ((attend[0], mix[0], units[0]), (mix[0], attend[1], moe_alone),
                                  (attend[1], mix[1], units[1]), (mix[1], None, moe_alone)):
            begun = done
            done = 0
            for _ in range(alone - begun):
                next(phase)
            while True:
                if nxt is not None:
                    next(nxt)
                    done += 1
                if next(phase, "end") == "end":
                    break
        sync.wait(t_out[-1])

        block = stack.enter_context(nc.Block())

        @block.sync
        def _(eng):
            sync.play(eng)

        @block.tensor
        def _(eng):
            pe.play(eng)

        @block.scalar
        def _(eng):
            act.play(eng)

        @block.vector
        def _(eng):
            dve.play(eng)

        @block.gpsimd
        def _(eng):
            pool.play(eng)


_INS = ["x", "ctx_1024", "g_xattn", "g_ffn",
        "L0_xattn_Wq", "L0_xattn_Wk", "L0_xattn_Wv", "L0_xattn_Wo", "L0_xattn_bo",
        "L0_ffn_Wr", "L0_ffn_br", "L0_ffn_Wl1", "L0_ffn_bl1", "L0_ffn_Wl2", "L0_ffn_bl2", "L0_ffn_biases_N",
        "L1_xattn_Wq", "L1_xattn_bq", "L1_xattn_Wk", "L1_xattn_bk", "L1_xattn_Wv", "L1_xattn_bv",
        "L1_xattn_Wo", "L1_xattn_bo", "L1_ffn_router_w", "L1_ffn_w1", "L1_ffn_w2"]


def kernel(**inputs):
    import numpy as _np
    import concourse.bacc as _bacc
    from concourse import mybir as _mybir
    from concourse.bass_utils import run_bass_kernel_spmd as _run

    nc = _bacc.Bacc("TRN2", target_bir_lowering=False, num_devices=1)
    arrays, args = {}, {}
    for name in _INS:
        arr = _np.ascontiguousarray(inputs[name])
        arrays[f"in_{name}_dram"] = arr
        args[name] = nc.dram_tensor(f"in_{name}_dram", arr.shape, _mybir.dt.from_np(arr.dtype),
                                    kind="ExternalInput").ap()
    shape = arrays["in_x_dram"].shape
    out = nc.dram_tensor("out_0_dram", shape, _mybir.dt.float32, kind="ExternalOutput").ap()
    flamingo_two_layers(nc, args, out)
    r = _run(nc, [arrays], core_ids=[0])
    return r.results[0]["out_0_dram"]
```
